# Optimizing a Trainium2 kernel written in Bass

```python
import numpy as np
import jax
import jax.numpy as jnp

def _softmax(x, axis=-1):
    return jax.nn.softmax(x, axis=axis)
def _gelu(x):
    return jax.nn.gelu(x, approximate=True)
def _silu(x):
    return jax.nn.silu(x)
def _sigmoid(x):
    return jax.nn.sigmoid(x)
def _layernorm(x, axis=-1, eps=1e-5):
    m = jnp.mean(x, axis=axis, keepdims=True)
    v = jnp.var(x, axis=axis, keepdims=True)
    return (x - m) / jnp.sqrt(v + eps)
def _scatter_add(tgt, idx, src, axis=0):
    return tgt.at[idx].add(src)
def _segment_sum(src, seg, n):
    return jax.ops.segment_sum(src, seg, n)

kernel_name = 'mk_conv_seq_d2_conv_nchw64_3ea80b'

def setup_inputs(seed: int = 0):
    np.random.seed(seed)
    _w = jnp.asarray
    def _rec_inputs():
        import jax
        import jax.numpy as jnp
        _gk = jax.random.key(seed)
        x = -7.109e-05 + 0.9999 * jax.random.normal(jax.random.fold_in(_gk, 1), (16, 64, 256, 256), jnp.float32)
        return x
    x = _rec_inputs()
    def _L0_conv_setup():
        import jax, jax.numpy as jnp
        import numpy as np
        B, C, H, W = (16, 64, 256, 256)
        MX, MY = (16, 16)
        GROUPS = 32
        EPS = 1e-05

        def _fno_layer(x, w1_re, w1_im, w2_re, w2_im, conv_w, conv_b, gn_w, gn_b):
            w1 = w1_re + 1j * w1_im
            w2 = w2_re + 1j * w2_im
            x_ft = jnp.fft.rfft2(x, axes=(-2, -1))
            top = jnp.einsum('bixy,ioxy->boxy', x_ft[:, :, :MX, :MY], w1)
            bot = jnp.einsum('bixy,ioxy->boxy', x_ft[:, :, H - MX:, :MY], w2)
            out_ft = jnp.zeros((B, C, H, W // 2 + 1), dtype=x_ft.dtype)
            out_ft = out_ft.at[:, :, :MX, :MY].set(top)
            out_ft = out_ft.at[:, :, H - MX:, :MY].set(bot)
            x_spec = jnp.fft.irfft2(out_ft, s=(H, W), axes=(-2, -1))
            x_loc = jnp.einsum('oi,bixy->boxy', conv_w, x) + conv_b[None, :, None, None]
            h = jax.nn.gelu(x_spec + x_loc + x, approximate=False)
            g = h.reshape(B, GROUPS, C // GROUPS, H, W)
            mu = g.mean(axis=(2, 3, 4), keepdims=True)
            var = g.var(axis=(2, 3, 4), keepdims=True)
            g = (g - mu) / jnp.sqrt(var + EPS)
            h = g.reshape(B, C, H, W)
            return h * gn_w[None, :, None, None] + gn_b[None, :, None, None]
        key = jax.random.key(seed)
        ks = jax.random.split(key, 9)
        scale = 1.0 / (C * C)
        f = lambda k, sh: jax.random.normal(k, sh, dtype=jnp.float32)
        return {'x': f(ks[0], (B, C, H, W)), 'w1_re': f(ks[1], (C, C, MX, MY)) * scale, 'w1_im': f(ks[2], (C, C, MX, MY)) * scale, 'w2_re': f(ks[3], (C, C, MX, MY)) * scale, 'w2_im': f(ks[4], (C, C, MX, MY)) * scale, 'conv_w': f(ks[5], (C, C)) * (1.0 / np.sqrt(C)), 'conv_b': f(ks[6], (C,)) * 0.01, 'gn_w': jnp.ones((C,), jnp.float32), 'gn_b': jnp.zeros((C,), jnp.float32)}
    _L0_conv_all = _L0_conv_setup()
    _L0_conv_in = {k: v for k, v in _L0_conv_all.items() if k in ('w1_re', 'w1_im', 'w2_re', 'w2_im', 'conv_w', 'conv_b', 'gn_w', 'gn_b', )}
    del _L0_conv_all

    def _L1_conv_setup():
        import jax, jax.numpy as jnp
        import numpy as np

        def fwht(x, axis):
            x = jnp.moveaxis(x, axis, -1)
            lead = x.shape[:-1]
            n = x.shape[-1]
            h = 1
            while h < n:
                x = x.reshape(lead + (n // (2 * h), 2, h))
                a = x[..., 0, :]
                b = x[..., 1, :]
                x = jnp.stack([a + b, a - b], axis=-2).reshape(lead + (n,))
                h *= 2
            return jnp.moveaxis(x, -1, axis)

        def ifwht(x, axis):
            n = x.shape[axis]
            return fwht(x, axis) / n

        def quaternion_weight(w_r, w_i, w_j, w_k):
            return jnp.concatenate([jnp.concatenate([w_r, -w_i, -w_j, -w_k], axis=1), jnp.concatenate([w_i, w_r, -w_k, w_j], axis=1), jnp.concatenate([w_j, w_k, w_r, -w_i], axis=1), jnp.concatenate([w_k, -w_j, w_i, w_r], axis=1)], axis=0)
        key = jax.random.key(seed)
        ks = jax.random.split(key, 6)
        B, C, H, W = (8, 64, 256, 256)
        c4 = C // 4
        return {'x': jax.random.normal(ks[0], (B, C, H, W), dtype=jnp.float32), 'w_r': jax.random.normal(ks[1], (c4, c4), dtype=jnp.float32) * 0.1, 'w_i': jax.random.normal(ks[2], (c4, c4), dtype=jnp.float32) * 0.1, 'w_j': jax.random.normal(ks[3], (c4, c4), dtype=jnp.float32) * 0.1, 'w_k': jax.random.normal(ks[4], (c4, c4), dtype=jnp.float32) * 0.1, 'T': jax.random.uniform(ks[5], (H, W), dtype=jnp.float32) / 10.0}
    _L1_conv_all = _L1_conv_setup()
    _L1_conv_in = {k: v for k, v in _L1_conv_all.items() if k in ('w_r', 'w_i', 'w_j', 'w_k', 'T', )}
    del _L1_conv_all

    return {
        "x": x,
        "L0_conv_w1_re": _L0_conv_in["w1_re"],
        "L0_conv_w1_im": _L0_conv_in["w1_im"],
        "L0_conv_w2_re": _L0_conv_in["w2_re"],
        "L0_conv_w2_im": _L0_conv_in["w2_im"],
        "L0_conv_conv_w": _L0_conv_in["conv_w"],
        "L0_conv_conv_b": _L0_conv_in["conv_b"],
        "L0_conv_gn_w": _L0_conv_in["gn_w"],
        "L0_conv_gn_b": _L0_conv_in["gn_b"],
        "L1_conv_w_r": _L1_conv_in["w_r"],
        "L1_conv_w_i": _L1_conv_in["w_i"],
        "L1_conv_w_j": _L1_conv_in["w_j"],
        "L1_conv_w_k": _L1_conv_in["w_k"],
        "L1_conv_T": _L1_conv_in["T"],
    }

def reference(x, L0_conv_w1_re, L0_conv_w1_im, L0_conv_w2_re, L0_conv_w2_im, L0_conv_conv_w, L0_conv_conv_b, L0_conv_gn_w, L0_conv_gn_b, L1_conv_w_r, L1_conv_w_i, L1_conv_w_j, L1_conv_w_k, L1_conv_T):
    import jax
    import jax.numpy as jnp
    def _L0_conv_ref(x, w1_re, w1_im, w2_re, w2_im, conv_w, conv_b, gn_w, gn_b):
        import jax, jax.numpy as jnp
        import numpy as np
        B, C, H, W = (16, 64, 256, 256)
        MX, MY = (16, 16)
        GROUPS = 32
        EPS = 1e-05

        def _fno_layer(x, w1_re, w1_im, w2_re, w2_im, conv_w, conv_b, gn_w, gn_b):
            w1 = w1_re + 1j * w1_im
            w2 = w2_re + 1j * w2_im
            x_ft = jnp.fft.rfft2(x, axes=(-2, -1))
            top = jnp.einsum('bixy,ioxy->boxy', x_ft[:, :, :MX, :MY], w1)
            bot = jnp.einsum('bixy,ioxy->boxy', x_ft[:, :, H - MX:, :MY], w2)
            out_ft = jnp.zeros((B, C, H, W // 2 + 1), dtype=x_ft.dtype)
            out_ft = out_ft.at[:, :, :MX, :MY].set(top)
            out_ft = out_ft.at[:, :, H - MX:, :MY].set(bot)
            x_spec = jnp.fft.irfft2(out_ft, s=(H, W), axes=(-2, -1))
            x_loc = jnp.einsum('oi,bixy->boxy', conv_w, x) + conv_b[None, :, None, None]
            h = jax.nn.gelu(x_spec + x_loc + x, approximate=False)
            g = h.reshape(B, GROUPS, C // GROUPS, H, W)
            mu = g.mean(axis=(2, 3, 4), keepdims=True)
            var = g.var(axis=(2, 3, 4), keepdims=True)
            g = (g - mu) / jnp.sqrt(var + EPS)
            h = g.reshape(B, C, H, W)
            return h * gn_w[None, :, None, None] + gn_b[None, :, None, None]
        return _fno_layer(x, w1_re, w1_im, w2_re, w2_im, conv_w, conv_b, gn_w, gn_b)

    def _L1_conv_ref(x, w_r, w_i, w_j, w_k, T):
        import jax, jax.numpy as jnp
        import numpy as np

        def fwht(x, axis):
            x = jnp.moveaxis(x, axis, -1)
            lead = x.shape[:-1]
            n = x.shape[-1]
            h = 1
            while h < n:
                x = x.reshape(lead + (n // (2 * h), 2, h))
                a = x[..., 0, :]
                b = x[..., 1, :]
                x = jnp.stack([a + b, a - b], axis=-2).reshape(lead + (n,))
                h *= 2
            return jnp.moveaxis(x, -1, axis)

        def ifwht(x, axis):
            n = x.shape[axis]
            return fwht(x, axis) / n

        def quaternion_weight(w_r, w_i, w_j, w_k):
            return jnp.concatenate([jnp.concatenate([w_r, -w_i, -w_j, -w_k], axis=1), jnp.concatenate([w_i, w_r, -w_k, w_j], axis=1), jnp.concatenate([w_j, w_k, w_r, -w_i], axis=1), jnp.concatenate([w_k, -w_j, w_i, w_r], axis=1)], axis=0)
        f = fwht(fwht(x, axis=-1), axis=-2)
        Wq = quaternion_weight(w_r, w_i, w_j, w_k)
        f = jnp.einsum('oc,bchw->bohw', Wq, f)
        f = jnp.sign(f) * jnp.maximum(jnp.abs(f) - T, 0.0)
        y = ifwht(ifwht(f, axis=-1), axis=-2)
        return y + x

    def _gn(v, G=32, eps=1e-5):
        B_, C_, H_, W_ = v.shape
        g = v.reshape(B_, G, C_ // G, H_, W_)
        m = jnp.mean(g, axis=(2, 3, 4), keepdims=True)
        s = jnp.var(g, axis=(2, 3, 4), keepdims=True)
        return ((g - m) / jnp.sqrt(s + eps)).reshape(v.shape)

    def _ln_c(v, eps=1e-6):
        m = jnp.mean(v, axis=1, keepdims=True)
        s = jnp.var(v, axis=1, keepdims=True)
        return (v - m) / jnp.sqrt(s + eps)

    def _ln_t(v, eps=1e-5):
        m = jnp.mean(v, axis=-1, keepdims=True)
        s = jnp.var(v, axis=-1, keepdims=True)
        return (v - m) / jnp.sqrt(s + eps)

    def _to_tokens(v):
        B_, C_, H_, W_ = v.shape
        return v.reshape(B_, C_, H_ * W_).transpose(0, 2, 1)
    def _from_tokens(t, like):
        B_, C_, H_, W_ = like.shape
        return t.transpose(0, 2, 1).reshape(B_, C_, H_, W_)

    x = _L0_conv_ref(x, L0_conv_w1_re, L0_conv_w1_im, L0_conv_w2_re, L0_conv_w2_im, L0_conv_conv_w, L0_conv_conv_b, L0_conv_gn_w, L0_conv_gn_b)
    x = _L1_conv_ref(x, L1_conv_w_r, L1_conv_w_i, L1_conv_w_j, L1_conv_w_k, L1_conv_T)
    return x


_drawn_inputs = setup_inputs


def setup_inputs(seed=0):
    import zlib

    import numpy as np

    out = dict(_drawn_inputs(seed))
    spreads = {'L0_conv_gn_w': (1.0, 0.2), 'L0_conv_gn_b': (0.0, 0.1)}
    factors = {'L0_conv_w1_re': 200.0,
     'L0_conv_w1_im': 200.0,
     'L0_conv_w2_re': 200.0,
     'L0_conv_w2_im': 200.0,
     'L0_conv_conv_b': 7.869,
     'L1_conv_T': 200.0}
    for name, (base, spread) in spreads.items():
        noise = np.random.default_rng([zlib.crc32(name.encode()), seed]).standard_normal(out[name].shape)
        drawn = base * np.exp(spread * noise) if base else spread * noise
        out[name] = jnp.asarray(drawn.astype(out[name].dtype))
    for name, factor in factors.items():
        out[name] = (out[name] * factor).astype(out[name].dtype)
    return out
```

```python
import math
from contextlib import ExitStack

import numpy as np
import concourse.bass as bass
from concourse import mybir

C, H, W = 64, 256, 256
P = 128
HL = H // 2
MODES = 16
NX = 2 * MODES
NP = 2 * MODES + 1
NPP = 64
NY = 2 * MODES
HW = H * W
GN_EPS = 1e-5

FP32 = mybir.dt.float32
BF16 = mybir.dt.bfloat16
ACT = mybir.ActivationFunctionType
ALU = mybir.AluOpType

UNIT = 1024
SLOTS = 4
ROWS = UNIT // W
ROW_UNITS = HL // ROWS
STEPS = C // 2
CHUNK_ROWS = 8
CHUNKS = HL // CHUNK_ROWS
SPILL_UNITS = 4
SPILLS = ROW_UNITS // SPILL_UNITS


def schedule():
    order, used = [], [0] * SLOTS

    def unit(kind, index, slot):
        order.append((kind, index, slot, used[slot]))
        used[slot] += 1

    for k in range(C // 4):
        unit("modes_to_rows", k, k % SLOTS)
    for k in range(ROW_UNITS):
        unit("conv", k, k % SLOTS)
    unit("group", 0, 0)
    for k in range(ROW_UNITS):
        unit("mix", k, k % SLOTS)
    for step in range(STEPS + 3):
        for slot, kind in enumerate(("fwd_w", "fwd_h", "inv_h", "inv_w")):
            if 0 <= step - slot < STEPS:
                unit(kind, step - slot, slot)
    return order, used


def use_of(order, kind, index):
    return next((slot, use) for k, i, slot, use in order if k == kind and i == index)


def forward_transform(nc, psum, x, spectrum_dram, w_fwd_h, w_fwd_w, identity, batch):
    GROUP = 8
    groups = batch * C // GROUP
    x_g = x.rearrange("b (g c) (t p) w -> (b g) p (c t) w", c=GROUP, p=P)
    out_g = spectrum_dram.rearrange("b (g c) m k -> (b g) m c k", c=GROUP)
    with ExitStack() as ctx:
        def sb(name, shape, dtype=FP32):
            return ctx.enter_context(nc.sbuf_tensor(name, shape, dtype))

        def sem(name):
            return ctx.enter_context(nc.semaphore(name))

        xin = sb("p1_x", [P, 2, 2 * GROUP, W])
        rows = sb("p1_rows", [P, 4, 512])
        cols = sb("p1_cols", [P, 2, 2, GROUP, NP])
        spec = sb("p1_spec", [NY, 2, GROUP * NP])
        x_in = [sem(f"p1_x_in{n}") for n in range(2)]
        h_done, h_copied = sem("p1_h_done"), sem("p1_h_copied")
        t_done, t_copied = sem("p1_t_done"), sem("p1_t_copied")
        w_done, w_copied = sem("p1_w_done"), sem("p1_w_copied")
        stored = [sem(f"p1_stored{n}") for n in range(2)]
        block = ctx.enter_context(nc.Block())

        @block.sync
        def _(sp):
            for n in range(2):
                sp.dma_start(xin[:, n], x_g[n]).then_inc(x_in[n], 16)
            with sp.Fori(1, groups // 2) as pair:
                g = 2 * pair
                for n in range(2):
                    sp.wait_ge(h_done, 2 * (g + n) - 2)
                    sp.dma_start(xin[:, n], x_g[g + n]).then_inc(x_in[n], 16)

        @block.tensor
        def _(pe):
            with pe.Fori(0, groups // 2) as pair:
                g = 2 * pair
                for n in range(2):
                    pe.wait_ge(x_in[n], 8 * g + 16)
                    for u in range(2):
                        pe.wait_ge(h_copied, 2 * (g + n) + u + 1)
                        for j in range(2):
                            for t in range(2):
                                c0 = 4 * u + 2 * j
                                both = xin[:, n, 2 * c0:2 * c0 + 4, :].rearrange("p (c t) w -> p t c w", t=2)
                                mm = pe.matmul(psum[NPP * j:NPP * j + NPP, 2 * n + u, :], w_fwd_h[:, t, :],
                                               both[:, t], start=(t == 0), stop=(t == 1))
                        mm.then_inc(h_done, 1)
                    for u in range(2):
                        pe.wait_ge(h_copied, 2 * (g + n) + u + 5)
                        pe.wait_ge(t_copied, 2 * (g + n) + u + 1)
                        for t in range(2):
                            for c in range(2):
                                q = 2 * t + c
                                piece = rows[:, 2 * n + u, W * c + P * t:W * c + P * t + P]
                                mm = pe.transpose(psum[:, 4 + u, P * q:P * q + P], piece, identity)
                        mm.then_inc(t_done, 1)
                    pe.wait_ge(t_copied, 2 * (g + n) + 4)
                    pe.wait_ge(w_copied, g + n + 1)
                    for t in range(2):
                        mm = pe.matmul(psum[0:NY, 6 + n, 0:GROUP * NP], w_fwd_w[:, t, :],
                                       cols[:, n, t].rearrange("p c k -> p (c k)"), start=(t == 0), stop=(t == 1))
                    mm.then_inc(w_done, 1)

        @block.scalar
        def _(act):
            act.sem_inc(h_copied, 4)
            act.sem_inc(w_copied, 2)
            for n in range(2):
                act.sem_inc(stored[n], 16)
            with act.Fori(0, groups // 2) as pair:
                g = 2 * pair
                for n in range(2):
                    for u in range(2):
                        act.wait_ge(h_done, 2 * (g + n) + u + 1)
                        act.activation(rows[:, 2 * n + u, :], psum[:, 2 * n + u, :], ACT.Copy).then_inc(h_copied, 1)
                    act.wait_ge(w_done, g + n + 1)
                    act.wait_ge(stored[n], 8 * g + 16)
                    act.activation(spec[:, n, :], psum[0:NY, 6 + n, 0:GROUP * NP], ACT.Copy).then_inc(w_copied, 1)
                    act.wait_ge(w_copied, g + n + 3)
                    act.dma_start(out_g[g + n], spec[:, n, :].rearrange("m (c k) -> m c k", k=NP)
                                  ).then_inc(stored[n], 16)
            for n in range(2):
                act.wait_ge(stored[n], 8 * groups + 16)

        @block.vector
        def _(dve):
            dve.sem_inc(t_copied, 2)
            with dve.Fori(0, groups // 2) as pair:
                g = 2 * pair
                for n in range(2):
                    for u in range(2):
                        dve.wait_ge(t_done, 2 * (g + n) + u + 1)
                        for t in range(2):
                            got = psum[:, 4 + u, 2 * P * t:2 * P * t + 2 * P].rearrange(
                                "p (c j k) -> p j c k", c=2, j=2)[:, :, :, 0:NP]
                            put = cols[:, n, t, 4 * u:4 * u + 4, :].rearrange("p (j c) k -> p j c k", j=2)
                            cp = dve.tensor_copy(put, got)
                        cp.then_inc(t_copied, 1)


def mix_modes(nc, psum, spectrum_dram, mixed_dram, w1_re, w1_im, w2_re, w2_im, part_sign, batch):
    XS = 4
    XY = XS * MODES
    chunks = NX // XS
    M = 2 * batch
    with ExitStack() as ctx:
        def sb(name, shape, dtype=FP32):
            return ctx.enter_context(nc.sbuf_tensor(name, shape, dtype))

        def sem(name):
            return ctx.enter_context(nc.semaphore(name))

        modes = sb("mm_modes", [P, 2, batch, NX, MODES])
        raw = sb("mm_raw", [P, 2, 2, MODES, NP])
        wts = sb("mm_wts", [P, 2, 2, C, XY])
        mixed = sb("mm_mixed", [M, 2, UNIT])
        raw_in = [sem(f"mm_raw_in{n}") for n in range(2)]
        raw_used = sem("mm_raw_used")
        negated_modes = sem("mm_negated_modes")
        w_in = [sem(f"mm_w_in{n}") for n in range(2)]
        w_negated = sem("mm_w_negated")
        u_done, u_copied = sem("mm_u_done"), sem("mm_u_copied")
        stored = [sem(f"mm_stored{n}") for n in range(2)]
        block = ctx.enter_context(nc.Block())
        units = chunks * 2 * XS

        @block.sync
        def _(sp):
            def load_raw(b, n):
                for half in range(2):
                    for plane in range(2):
                        part = plane if half == 0 else 1 - plane
                        sp.dma_start(raw[C * half:C * half + C, n, plane].rearrange("p y k -> p (y k)"),
                                     spectrum_dram[b, :, MODES * part:MODES * part + MODES, :].rearrange(
                                         "c m k -> c (m k)")).then_inc(raw_in[n], 16)
            for b in range(batch):
                if b >= 2:
                    sp.wait_ge(raw_used, b - 1)
                load_raw(b, b % 2)

        @block.gpsimd
        def _(pool):
            for k in range(chunks):
                if k >= 2:
                    pool.wait_ge(u_done, 2 * XS * (k - 1))
                first = k * XS < MODES
                re, im = (w1_re, w1_im) if first else (w2_re, w2_im)
                x0 = k * XS if first else 2 * MODES - (k + 1) * XS
                for half in range(2):
                    for part, src in enumerate((re, im) if half == 0 else (im, re)):
                        pool.dma_start(wts[C * half:C * half + C, k % 2, part],
                                       src[:, :, x0:x0 + XS, :].rearrange("i o x y -> i o (x y)")
                                       ).then_inc(w_in[k % 2], 16)

        @block.vector
        def _(dve):
            def negate(k):
                dve.wait_ge(w_in[k % 2], 64 * (k // 2 + 1))
                w = wts[C:P, k % 2, 0].rearrange("p o q -> p (o q)")
                dve.tensor_scalar(w, w, -1.0, None, ALU.mult).then_inc(w_negated, 1)

            for b in range(batch):
                n = b % 2
                dve.wait_ge(raw_in[n], 64 * (b // 2 + 1))
                cos, sin = raw[:, n, 0], raw[:, n, 1]
                dve.tensor_copy(modes[:, 0, b, 0, :], cos[:, :, 0])
                for plus in range(2):
                    last = MODES if plus else MODES + 1
                    q0 = 1 if plus else MODES
                    put = modes[:, 0, b, q0:q0 + last - 1, :].rearrange("p q y -> p y q")
                    op = dve.scalar_tensor_tensor(put, sin[:, :, MODES + 1:MODES + last],
                                                  part_sign[:, 1 - plus:2 - plus], cos[:, :, 1:last],
                                                  ALU.mult, ALU.add)
                op.then_inc(raw_used, 1)
            dve.wait_ge(raw_used, batch)
            dve.tensor_scalar(modes[:, 1].rearrange("p b q y -> p (b q y)"),
                              modes[:, 0].rearrange("p b q y -> p (b q y)"), -1.0, None, ALU.mult
                              ).then_inc(negated_modes, 1)
            for k in range(chunks):
                negate(k)

        @block.tensor
        def _(pe):
            pe.wait_ge(negated_modes, 1)
            for k in range(chunks):
                pe.wait_ge(w_negated, k + 1)
                for xi in range(XS):
                    q = k * XS + xi
                    x_local = xi if q < MODES else XS - 1 - xi
                    for yh in range(2):
                        u = 2 * q + yh
                        if u >= SLOTS:
                            pe.wait_ge(u_copied, u - SLOTS + 1)
                        for y8 in range(8):
                            y = 8 * yh + y8
                            bank = 2 * (u % SLOTS) + y8 // 4
                            mm = pe.matmul(psum[0:M, bank, P * (y8 % 4):P * (y8 % 4) + P],
                                           modes[:, :, :, q, y].rearrange("p s b -> p (s b)"),
                                           wts[:, k % 2, :, :, MODES * x_local + y].rearrange("p r o -> p (r o)"),
                                           start=True, stop=True)
                        mm.then_inc(u_done, 1)

        @block.scalar
        def _(act):
            out = mixed_dram.rearrange("s b q y r o -> (s b) (q y r o)")
            for u in range(units):
                act.wait_ge(u_done, u + 1)
                if u >= 2:
                    act.wait_ge(stored[u % 2], 16 * (u // 2))
                slot = 2 * (u % SLOTS)
                act.activation(mixed[:, u % 2, :], psum[0:M, slot:slot + 2, :].rearrange("p a q -> p (a q)"),
                               ACT.Copy).then_inc(u_copied, 1)
                act.wait_ge(u_copied, u + 1)
                act.dma_start(out[:, UNIT * u:UNIT * u + UNIT], mixed[:, u % 2, :]).then_inc(stored[u % 2], 16)
            for n in range(2):
                act.wait_ge(stored[n], 16 * (units // 2))


def images(nc, psum, x, mixed_dram, normed_dram, y_out, k, batch):
    order, used = schedule()
    x_c = x.rearrange("b c (f r) w -> b f c (r w)", f=2)
    normed_c = normed_dram.rearrange("b c (f r) w -> b f c (r w)", f=2)
    normed_r = normed_dram.rearrange("b (s o) (f p) w -> b s p (o f) w", p=P, o=2)
    y_r = y_out.rearrange("b (s o) (f p) w -> b s p (o f) w", p=P, o=2)
    with ExitStack() as ctx:
        def sb(name, shape, dtype=FP32):
            return ctx.enter_context(nc.sbuf_tensor(name, shape, dtype))

        def sem(name):
            return ctx.enter_context(nc.semaphore(name))

        image = sb("image", [P, HL * W])
        spec_rows = image[0:NY, HL * W // 2:].rearrange("p (r f o) -> p o f r", f=2, o=C)
        mixed = image[:, :].rearrange("p (r t m) -> p t m r", t=2, m=P)
        xin = sb("xin", [P, 2, CHUNK_ROWS * W])
        kept = k["kept"]
        along_w = sb("along_w", [P, 2, UNIT])
        freq = sb("freq", [P, 2, UNIT])
        along_h = sb("along_h", [P, 2, 2, 2, H])
        over = sb("over", [P, UNIT])
        sign = sb("sign", [P, UNIT], BF16)
        resid = sb("resid", [P, 2, UNIT])
        yout = sb("yout", [P, 2, UNIT])
        parts = sb("parts", [P, 2 * ROW_UNITS, 6])
        st = sb("st", [P, 12])
        gelu_bias, gn_w, gn_b = k["cols"][:, 0:1], k["cols"][:, 1:2], k["cols"][:, 2:3]

        x_in = [sem(f"x_in{n}") for n in range(2)]
        x_used = sem("x_used")
        kept_in, kept_used = sem("kept_in"), sem("kept_used")
        full = [sem(f"slot{n}_full") for n in range(SLOTS)]
        copied = [sem(f"slot{n}_copied") for n in range(SLOTS)]
        stats_ready = sem("stats_ready")
        rooted = sem("rooted")
        normed = sem("normed")
        spilled = [sem(f"spilled{n}") for n in range(SPILLS)]
        signed = sem("signed")
        over_made = sem("over_made")
        r_in = [sem(f"resid_in{n}") for n in range(2)]
        y_stored = [sem(f"y_stored{n}") for n in range(2)]
        chain = sem("vector_chain")
        block = ctx.enter_context(nc.Block())

        def filled(b, slot, use):
            return b * used[slot] + use + 1

        def freed(b, slot, use):
            return b * used[slot] + use + 1

        def in_sbuf(b, kind, index):
            slot, use = use_of(order, kind, index)
            return copied[slot], b * used[slot] + use + 2

        def slot_cols(slot):
            return psum[:, 2 * slot:2 * slot + 2, :].rearrange("p a q -> p (a q)")

        @block.gpsimd
        def _(pool):
            with pool.Fori(0, batch) as b:
                pool.wait_ge(kept_used, b + 1)
                for part in range(2):
                    for r in range(2):
                        src = (0, r) if part == 0 else ((1, 1) if r == 0 else (0, 0))
                        pool.dma_start(kept[NX * part:NX * part + NX, :, r, :],
                                       mixed_dram[src[0], b, :, :, src[1], :]).then_inc(kept_in, 16)
                for c in range(CHUNKS):
                    n = c % 2
                    pool.wait_ge(x_used, b * CHUNKS + c + 1)
                    for f in range(2):
                        pool.dma_start(xin[C * f:C * f + C, n, :],
                                       x_c[b, f, :, CHUNK_ROWS * W * c:CHUNK_ROWS * W * (c + 1)]
                                       ).then_inc(x_in[n], 16)

        @block.sync
        def _(sp):
            for n in range(2):
                sp.sem_inc(y_stored[n], 16)
            with sp.Fori(0, batch) as b:
                for s in range(SPILLS):
                    sp.wait_ge(normed, b * SPILLS + s + 1)
                    q = SPILL_UNITS * UNIT
                    for f in range(2):
                        sp.dma_start(normed_c[b, f, :, q * s:q * s + q],
                                     image[C * f:C * f + C, q * s:q * s + q]).then_inc(spilled[s], 16)
                for s in range(SPILLS):
                    sp.wait_ge(spilled[s], 32 * b + 32)
                for s in range(STEPS + 1):
                    if s < STEPS:
                        if s >= 2:
                            sp.wait_ge(*in_sbuf(b, "inv_w", s - 2))
                        sp.dma_start(resid[:, s % 2, :].rearrange("p (a w) -> p a w", w=W),
                                     normed_r[b, s]).then_inc(r_in[s % 2], 16)
                    if s >= 1:
                        sp.wait_ge(*in_sbuf(b, "inv_w", s - 1))
                        sp.dma_start(y_r[b, s - 1], yout[:, (s - 1) % 2, :].rearrange("p (a w) -> p a w", w=W)
                                     ).then_inc(y_stored[(s - 1) % 2], 16)
            for n in range(2):
                sp.wait_ge(y_stored[n], 8 * batch * STEPS + 16)

        @block.tensor
        def _(pe):
            pe.sem_inc(kept_used, 1)
            pe.sem_inc(x_used, 2)
            with pe.Fori(0, batch) as b:
                for kind, i, slot, use in order:
                    pe.wait_ge(copied[slot], freed(b, slot, use))
                    bank = 2 * slot
                    if kind == "modes_to_rows":
                        if i == 0:
                            pe.wait_ge(kept_in, 64 * b + 64)
                        for o in range(4):
                            mm = pe.matmul(psum[0:NY, bank + o // 2, W * (o % 2):W * (o % 2) + W],
                                           kept[:, :, :, 4 * i + o].rearrange("p y r -> p (y r)"),
                                           k["inv_h"], start=True, stop=True)
                    elif kind == "conv":
                        if i == 0:
                            for q in range(C // 4 - SLOTS, C // 4):
                                pe.wait_ge(*in_sbuf(b, "modes_to_rows", q))
                        c = i // 2
                        if i % 2 == 0:
                            pe.wait_ge(x_in[c % 2], 32 * (b * (CHUNKS // 2) + c // 2 + 1))
                        for pair in range(2):
                            for r in range(2):
                                at = UNIT * (i % 2) + 512 * pair + W * r
                                mm = pe.matmul(psum[:, bank + pair, W * r:W * r + W], k["conv"],
                                               xin[:, c % 2, at:at + W], start=True, stop=False)
                                if i == 0 and pair == 0 and r == 0:
                                    mm.then_inc(kept_used, 1)
                                if i % 2 == 1 and pair == 1 and r == 1:
                                    mm.then_inc(x_used, 1)
                                row = ROWS * i + 2 * pair + r
                                base = HL * W // 2 + P * row
                                mm = pe.matmul(psum[:, bank + pair, W * r:W * r + W],
                                               image[0:NY, base:base + P], k["inv_w"],
                                               start=False, stop=True)
                    elif kind == "group":
                        pe.wait_ge(stats_ready, b + 1)
                        mm = pe.matmul(psum[:, bank, 0:2], k["group"], st[:, 2:4], start=True, stop=True)
                    elif kind == "mix":
                        if i % SPILL_UNITS == 0:
                            pe.wait_ge(normed, b * SPILLS + i // SPILL_UNITS + 1)
                        for q in range(8):
                            at = UNIT * i + P * q
                            mm = pe.matmul(psum[:, bank + q // 4, P * (q % 4):P * (q % 4) + P],
                                           image[:, at:at + P], k["mix"], start=True, stop=True)
                    elif kind == "fwd_w":
                        if i == 0:
                            for q in range(ROW_UNITS - SLOTS, ROW_UNITS):
                                pe.wait_ge(*in_sbuf(b, "mix", q))
                        for o in range(2):
                            for f in range(2):
                                for t in range(2):
                                    mm = pe.matmul(psum[:, bank + o, W * f:W * f + W],
                                                   mixed[:, t, C * f + 2 * i + o, :], k["wht"][:, t, :],
                                                   start=(t == 0), stop=(t == 1))
                    elif kind == "fwd_h":
                        pe.wait_ge(*in_sbuf(b, "fwd_w", i))
                        for o in range(2):
                            mm = pe.matmul(psum[:, bank + o, :], k["wht"][:, 0, 0:P],
                                           along_w[:, i % 2, 512 * o:512 * o + 512], start=True, stop=True)
                    elif kind == "inv_h":
                        pe.wait_ge(*in_sbuf(b, "fwd_h", i))
                        for o in range(2):
                            for t in range(2):
                                for f in range(2):
                                    at = 512 * o + W * f + P * t
                                    mm = pe.matmul(psum[:, bank + o, H * t:H * t + H],
                                                   freq[:, i % 2, at:at + P], k["wht"][:, f, :],
                                                   start=(f == 0), stop=(f == 1))
                    elif kind == "inv_w":
                        pe.wait_ge(*in_sbuf(b, "inv_h", i))
                        for o in range(2):
                            for f in range(2):
                                for t in range(2):
                                    mm = pe.matmul(psum[:, bank + o, W * f:W * f + W],
                                                   along_h[:, i % 2, o, t, P * f:P * f + P], k["wht"][:, t, :],
                                                   start=(t == 0), stop=(t == 1))
                    mm.then_inc(full[slot], 1)

        @block.scalar
        def _(act):
            for n in range(SLOTS):
                act.sem_inc(copied[n], 1)
            with act.Fori(0, batch) as b:
                for kind, i, slot, use in order:
                    if kind in ("inv_w", "fwd_h") or kind == "group" or (kind == "modes_to_rows" and i % 2):
                        if kind == "group":
                            act.wait_ge(rooted, 2 * b + 1)
                            act.activation(st[:, 5:6], st[:, 4:5], ACT.Sqrt).then_inc(rooted, 1)
                        if kind == "fwd_h":
                            act.wait_ge(full[slot], filled(b, slot, use))
                            act.activation(over[:, :], slot_cols(slot), ACT.Abs)
                            act.activation(sign[:, :], slot_cols(slot), ACT.Sign).then_inc(signed, 1)
                        continue
                    act.wait_ge(full[slot], filled(b, slot, use))
                    if kind == "modes_to_rows":
                        out = act.activation(spec_rows[:, 4 * i:4 * i + 4],
                                             slot_cols(slot)[0:NY].rearrange("p (o f r) -> p o f r", o=4, f=2),
                                             ACT.Copy)
                    elif kind == "conv":
                        out = act.activation(image[:, UNIT * i:UNIT * i + UNIT], slot_cols(slot), ACT.Gelu,
                                             bias=gelu_bias)
                    elif kind == "mix":
                        if i % SPILL_UNITS == 0:
                            act.wait_ge(spilled[i // SPILL_UNITS], 32 * b + 32)
                        out = act.activation(image[:, UNIT * i:UNIT * i + UNIT], slot_cols(slot), ACT.Copy)
                    elif kind == "fwd_w":
                        out = act.activation(along_w[:, i % 2, :], slot_cols(slot), ACT.Copy)
                    elif kind == "inv_h":
                        out = act.activation(along_h[:, i % 2].rearrange("p o t h -> p (o t h)"),
                                             slot_cols(slot), ACT.Copy)
                    out.then_inc(copied[slot], 1)

        @block.vector
        def _(dve):
            LINKS = 9

            with dve.Fori(0, batch) as b:
                links = 0

                def link(op):
                    nonlocal links
                    links += 1
                    op.then_inc(chain, 1)
                    dve.wait_ge(chain, b * LINKS + links)

                for kind, i, slot, use in order:
                    if kind == "modes_to_rows" and i % 2:
                        dve.wait_ge(full[slot], filled(b, slot, use))
                        dve.tensor_copy(spec_rows[:, 4 * i:4 * i + 4],
                                        slot_cols(slot)[0:NY].rearrange("p (o f r) -> p o f r", o=4, f=2)
                                        ).then_inc(copied[slot], 1)
                    elif kind == "conv":
                        dve.wait_ge(*in_sbuf(b, "conv", i))
                        for q in range(2):
                            at = UNIT * i + 512 * q
                            op = dve.bn_stats(parts[:, 2 * i + q, :], image[:, at:at + 512])
                        if i == ROW_UNITS - 1:
                            link(op)
                            dve.memset(st[:, 11:12], GN_EPS)
                            link(dve.bn_aggr(st[:, 0:2], parts[:, :, :].rearrange("p a s -> p (a s)")))
                            link(dve.tensor_tensor(st[:, 6:7], st[:, 0:1], st[:, 0:1], ALU.mult))
                            dve.tensor_copy(st[:, 2:3], st[:, 0:1])
                            dve.tensor_tensor(st[:, 3:4], st[:, 1:2], st[:, 6:7], ALU.add).then_inc(stats_ready, 1)
                    elif kind == "group":
                        dve.wait_ge(full[slot], filled(b, slot, use))
                        dve.tensor_copy(st[:, 7:9], psum[:, 2 * slot, 0:2]).then_inc(copied[slot], 1)
                        dve.wait_ge(*in_sbuf(b, "group", 0))
                        link(dve.tensor_tensor(st[:, 6:7], st[:, 7:8], st[:, 7:8], ALU.mult))
                        link(dve.tensor_tensor(st[:, 6:7], st[:, 8:9], st[:, 6:7], ALU.subtract))
                        dve.scalar_tensor_tensor(st[:, 4:5], st[:, 6:7], 0.0, st[:, 11:12], ALU.max, ALU.add
                                                 ).then_inc(rooted, 1)
                        dve.wait_ge(rooted, 2 * b + 2)
                        link(dve.reciprocal(st[:, 6:7], st[:, 5:6]))
                        link(dve.tensor_tensor(st[:, 9:10], st[:, 6:7], gn_w, ALU.mult))
                        link(dve.tensor_tensor(st[:, 6:7], st[:, 7:8], st[:, 9:10], ALU.mult))
                        link(dve.tensor_tensor(st[:, 10:11], gn_b, st[:, 6:7], ALU.subtract))
                        for s in range(SPILLS):
                            q = SPILL_UNITS * UNIT
                            rows = image[:, q * s:q * s + q]
                            dve.tensor_scalar(rows, rows, st[:, 9:10], st[:, 10:11], ALU.mult, ALU.add
                                              ).then_inc(normed, 1)
                    elif kind == "fwd_h":
                        dve.wait_ge(signed, b * STEPS + i + 1)
                        both = over[:, :].rearrange("p (o q) -> p o q", o=2)
                        dve.tensor_tensor(both, both, k["thr"].unsqueeze(1).broadcast_to([P, 2, 2 * W]),
                                          ALU.subtract).then_inc(over_made, 1)
                        dve.wait_ge(over_made, b * STEPS + i + 1)
                        dve.scalar_tensor_tensor(freq[:, i % 2, :], over[:, :], 0.0, sign[:, :], ALU.max,
                                                 ALU.mult).then_inc(copied[slot], 1)
                    elif kind == "inv_w":
                        dve.wait_ge(full[slot], filled(b, slot, use))
                        dve.wait_ge(r_in[i % 2], 16 * (b * (STEPS // 2) + i // 2 + 1))
                        dve.wait_ge(y_stored[i % 2], 16 * (b * (STEPS // 2) + i // 2 + 1))
                        dve.scalar_tensor_tensor(yout[:, i % 2, :], slot_cols(slot), 1.0 / HW, resid[:, i % 2, :],
                                                 ALU.mult, ALU.add).then_inc(copied[slot], 1)
                assert links == LINKS


def build(nc, a, out, batch):
    with ExitStack() as ctx:
        def sb(name, shape, dtype=FP32):
            return ctx.enter_context(nc.sbuf_tensor(name, shape, dtype))

        spectrum = nc.dram_tensor("spectrum", [batch, C, NY, NP], FP32, kind="Internal").ap()
        mixed_modes = nc.dram_tensor("mixed_modes", [2, batch, NX, MODES, 2, C], FP32, kind="Internal").ap()
        normed = nc.dram_tensor("normed", [batch, C, H, W], FP32, kind="Internal").ap()
        psum = ctx.enter_context(nc.psum_tensor("psum", [P, 8, 512], FP32))
        wht = sb("c_wht", [P, 2, W])
        thr = sb("c_thr", [P, 2 * W])
        conv = sb("c_conv", [P, P])
        mix = sb("c_mix", [P, P])
        group = sb("c_group", [P, P])
        inv_w = sb("c_inv_w", [NY, W])
        inv_h = sb("c_inv_h", [P, H])
        kept = sb("kept", [P, MODES, 2, C])
        cols = sb("c_cols", [P, 3])

        with ExitStack() as early:
            def eb(name, shape):
                return early.enter_context(nc.sbuf_tensor(name, shape, FP32))

            fwd_h = eb("c_fwd_h", [P, 2, NPP])
            fwd_w = eb("c_fwd_w", [P, 2, NY])
            identity = eb("c_identity", [P, P])
            mix_sign = eb("c_mix_sign", [P, P])
            part_sign = eb("c_part_sign", [P, 2])
            with nc.semaphore("c_in") as c_in, nc.semaphore("c_zero") as c_zero, \
                    nc.semaphore("c_made") as c_made, nc.Block() as block:
                loads = [
                    (fwd_h[:, :, :], a["k_fwd_h"]), (fwd_w[:, :, :], a["k_fwd_w"]),
                    (identity[:, :], a["k_identity"]), (mix_sign[:, :], a["k_mix_sign"]),
                    (part_sign[:, :], a["k_part_sign"]), (wht[:, :, :], a["k_wht"]),
                    (group[:, :], a["k_group"]), (inv_w[:, :], a["k_inv_w"]), (inv_h[:, :], a["k_inv_h"]),
                    (thr[:, :].rearrange("p (f w) -> p f w", f=2), a["T"].rearrange("(f p) w -> p f w", p=P)),
                ]
                for f in range(2):
                    half = slice(C * f, C * f + C)
                    loads.append((conv[half, C * f:C * f + C], a["conv_w_t"]))
                    for g in range(2):
                        loads.append((mix[half, C * g:C * g + C], a["mix_w_t"]))
                    for n, name in enumerate(("conv_b", "gn_w", "gn_b")):
                        loads.append((cols[half, n:n + 1], a[name].rearrange("(c n) -> c n", n=1)))

                @block.sync
                def _(sp):
                    sp.wait_ge(c_zero, 1)
                    for to, source in loads:
                        sp.dma_start(to, source).then_inc(c_in, 16)

                @block.vector
                def _(dve):
                    dve.memset(kept[2 * NX:, :, :, :], 0.0)
                    dve.memset(conv[:, :], 0.0).then_inc(c_zero, 1)
                    dve.wait_ge(c_in, 16 * len(loads))
                    dve.tensor_tensor(conv[:, :], conv[:, :], identity[:, :], ALU.add).then_inc(c_made, 1)
                    dve.tensor_tensor(mix[:, :], mix[:, :], mix_sign[:, :], ALU.mult).then_inc(c_made, 1)
                    dve.wait_ge(c_made, 2)

            forward_transform(nc, psum, a["x"], spectrum, fwd_h, fwd_w, identity[:, :], batch)
            mix_modes(nc, psum, spectrum, mixed_modes, a["w1_re"], a["w1_im"], a["w2_re"], a["w2_im"],
                      part_sign, batch)
        consts = {"wht": wht, "thr": thr[:, :], "conv": conv[:, :], "mix": mix[:, :], "group": group[:, :],
                  "inv_w": inv_w[:, :], "inv_h": inv_h[:, :], "cols": cols,
                  "kept": kept}
        images(nc, psum, a["x"], mixed_modes, normed, out, consts, batch)


def constants():
    h = np.arange(H)
    angle = 2 * np.pi / H * np.outer(h, np.arange(MODES + 1))
    fwd_h = np.zeros((H, NPP))
    fwd_h[:, :MODES + 1] = np.cos(angle)
    fwd_h[:, MODES + 1:NP] = np.sin(angle[:, 1:])
    angle = 2 * np.pi / W * np.outer(np.arange(W), np.arange(MODES))
    fwd_w = np.concatenate([np.cos(angle), -np.sin(angle)], axis=1)
    freqs = np.array([q if q < MODES else MODES - 1 - q for q in range(NX)])
    angle = 2 * np.pi / H * np.outer(freqs, h)
    inv_h = np.concatenate([np.cos(angle), np.sin(angle), np.zeros((P - 2 * NX, H))])
    ky = np.arange(MODES)
    angle = 2 * np.pi / W * np.outer(ky, np.arange(W))
    twice = np.where(ky == 0, 1.0, 2.0)[:, None] / HW
    inv_w = np.stack([twice * np.cos(angle), -twice * np.sin(angle)], axis=1).reshape(NY, W)
    wht = np.array([[1.0]])
    while wht.shape[0] < H:
        wht = np.block([[wht, wht], [wht, -wht]])
    quaternion = np.array([[1, -1, -1, -1], [1, 1, -1, 1], [1, 1, 1, -1], [1, -1, 1, 1]])
    sign = np.kron(quaternion.T, np.ones((C // 4, C // 4)))
    row = np.arange(P)
    same = (row[:, None] % C // 2) == (row[None, :] % C // 2)
    part = np.where(row < C, 1.0, -1.0)
    split = lambda m: m.reshape(2, P, -1).transpose(1, 0, 2)
    made = {
        "k_fwd_h": split(fwd_h), "k_fwd_w": split(fwd_w), "k_identity": np.eye(P),
        "k_mix_sign": np.block([[sign, sign], [sign, -sign]]), "k_part_sign": np.stack([part, -part], axis=1),
        "k_wht": split(wht), "k_group": same / 4.0, "k_inv_w": inv_w, "k_inv_h": inv_h,
    }
    return {name: np.ascontiguousarray(m, dtype=np.float32) for name, m in made.items()}


def layout(inputs):
    a = {"x": inputs["x"], "T": inputs["L1_conv_T"]}
    for name in ("w1_re", "w1_im", "w2_re", "w2_im", "conv_b", "gn_w", "gn_b"):
        a[name] = inputs["L0_conv_" + name]
    a["conv_w_t"] = np.asarray(inputs["L0_conv_conv_w"]).T
    r, i, j, k = (np.asarray(inputs["L1_conv_w_" + n]).T for n in "rijk")
    a["mix_w_t"] = np.block([[r, i, j, k], [i, r, k, j], [j, k, r, i], [k, j, i, r]])
    return {name: np.ascontiguousarray(v) for name, v in a.items()} | constants()


def kernel(**inputs):
    import concourse.bacc as bacc
    from concourse.bass_utils import run_bass_kernel_spmd

    a = layout(inputs)
    batch = a["x"].shape[0]
    nc = bacc.Bacc("TRN2", target_bir_lowering=False, num_devices=1)
    aps = {n: nc.dram_tensor(n, v.shape, mybir.dt.from_np(v.dtype), kind="ExternalInput").ap() for n, v in a.items()}
    out = nc.dram_tensor("y", (batch, C, H, W), FP32, kind="ExternalOutput").ap()
    build(nc, aps, out, batch)
    result = run_bass_kernel_spmd(nc, [a], core_ids=[0])
    return result.results[0]["y"]
```

```python
import math
from contextlib import ExitStack

import numpy as np
import concourse.bass as bass
from concourse import mybir

C, H, W = 64, 256, 256
P = 128
HL = H // 2
MODES = 16
NX = 2 * MODES
NP = 2 * MODES + 1
NPP = 64
NY = 2 * MODES
HW = H * W
GN_EPS = 1e-5

FP32 = mybir.dt.float32
FP32R = mybir.dt.float32r
BF16 = mybir.dt.bfloat16
ACT = mybir.ActivationFunctionType
ALU = mybir.AluOpType

UNIT = 1024
SLOTS = 4
ROWS = UNIT // W
ROW_UNITS = HL // ROWS
STEPS = C // 2
X_BUFS = 3
KEPT_O = 16
KEPTS = C // KEPT_O
SPILL_UNITS = 4
SPILLS = ROW_UNITS // SPILL_UNITS


def schedule():
    order, used = [], [0] * SLOTS

    def unit(kind, index, slot):
        order.append((kind, index, slot, used[slot]))
        used[slot] += 1

    for k in range(C // 4):
        unit("modes_to_rows", k, k % SLOTS)
    for k in range(ROW_UNITS):
        unit("conv", k, k % SLOTS)
    unit("group", 0, 0)
    for k in range(ROW_UNITS):
        unit("mix", k, k % SLOTS)
    for step in range(STEPS + 3):
        for slot, kind, lag in ((1, "fwd_h", 1), (0, "fwd_w", 0), (3, "inv_w", 3), (2, "inv_h", 2)):
            if 0 <= step - lag < STEPS:
                unit(kind, step - lag, slot)
    return order, used


def use_of(order, kind, index):
    return next((slot, use) for k, i, slot, use in order if k == kind and i == index)


def forward_transform(nc, psum, x, spectrum_dram, w_fwd_h, w_fwd_w, identity, batch):
    GROUP = 8
    BUFS = 4
    groups = batch * C // GROUP
    x_g = x.rearrange("b (g c) (t p) w -> (b g) p (c t) w", c=GROUP, p=P)
    out_g = spectrum_dram.rearrange("b (g c) m k -> (b g) m c k", c=GROUP)
    with ExitStack() as ctx:
        def sb(name, shape, dtype=FP32):
            return ctx.enter_context(nc.sbuf_tensor(name, shape, dtype))

        def sem(name):
            return ctx.enter_context(nc.semaphore(name))

        xin = sb("p1_x", [P, BUFS, 2 * GROUP, W])
        rows = sb("p1_rows", [P, 4, 512])
        cols = sb("p1_cols", [P, 2, 2, GROUP, NP])
        spec = sb("p1_spec", [NY, 2, GROUP * NP])
        x_in = [sem(f"p1_x_in{n}") for n in range(BUFS)]
        h_done, h_copied = sem("p1_h_done"), sem("p1_h_copied")
        t_done, t_copied = sem("p1_t_done"), sem("p1_t_copied")
        w_done, w_copied = sem("p1_w_done"), sem("p1_w_copied")
        stored = [sem(f"p1_stored{n}") for n in range(2)]
        block = ctx.enter_context(nc.Block())

        @block.sync
        def _(sp):
            for n in range(BUFS):
                sp.dma_start(xin[:, n], x_g[n]).then_inc(x_in[n], 16)
            with sp.Fori(1, groups // BUFS) as turn:
                g = BUFS * turn
                for n in range(BUFS):
                    sp.wait_ge(h_done, 2 * (g + n + 1 - BUFS))
                    sp.dma_start(xin[:, n], x_g[g + n]).then_inc(x_in[n], 16)

        @block.tensor
        def _(pe):
            with pe.Fori(0, groups // BUFS) as turn:
                for m in range(BUFS):
                    g, n = BUFS * turn + m - m % 2, m % 2
                    pe.wait_ge(x_in[m], 16 * turn + 16)
                    for u in range(2):
                        pe.wait_ge(h_copied, 2 * (g + n) + u + 1)
                        for j in range(2):
                            for t in range(2):
                                c0 = 4 * u + 2 * j
                                both = xin[:, m, 2 * c0:2 * c0 + 4, :].rearrange("p (c t) w -> p t c w", t=2)
                                mm = pe.matmul(psum[NPP * j:NPP * j + NPP, 2 * n + u, :], w_fwd_h[:, t, :],
                                               both[:, t], start=(t == 0), stop=(t == 1))
                        mm.then_inc(h_done, 1)
                    for u in range(2):
                        pe.wait_ge(h_copied, 2 * (g + n) + u + 5)
                        pe.wait_ge(t_copied, 2 * (g + n) + u + 1)
                        for t in range(2):
                            for c in range(2):
                                q = 2 * t + c
                                piece = rows[:, 2 * n + u, W * c + P * t:W * c + P * t + P]
                                mm = pe.transpose(psum[:, 4 + u, P * q:P * q + P], piece, identity)
                        mm.then_inc(t_done, 1)
                    pe.wait_ge(t_copied, 2 * (g + n) + 4)
                    pe.wait_ge(w_copied, g + n + 1)
                    for t in range(2):
                        mm = pe.matmul(psum[0:NY, 6 + n, 0:GROUP * NP], w_fwd_w[:, t, :],
                                       cols[:, n, t].rearrange("p c k -> p (c k)"), start=(t == 0), stop=(t == 1))
                    mm.then_inc(w_done, 1)

        @block.scalar
        def _(act):
            act.sem_inc(h_copied, 4)
            act.sem_inc(w_copied, 2)
            for n in range(2):
                act.sem_inc(stored[n], 16)
            with act.Fori(0, groups // 2) as pair:
                g = 2 * pair
                for n in range(2):
                    for u in range(2):
                        act.wait_ge(h_done, 2 * (g + n) + u + 1)
                        act.activation(rows[:, 2 * n + u, :], psum[:, 2 * n + u, :], ACT.Copy).then_inc(h_copied, 1)
                    act.wait_ge(w_done, g + n + 1)
                    act.wait_ge(stored[n], 8 * g + 16)
                    act.activation(spec[:, n, :], psum[0:NY, 6 + n, 0:GROUP * NP], ACT.Copy).then_inc(w_copied, 1)
                    act.wait_ge(w_copied, g + n + 3)
                    act.dma_start(out_g[g + n], spec[:, n, :].rearrange("m (c k) -> m c k", k=NP)
                                  ).then_inc(stored[n], 16)
            for n in range(2):
                act.wait_ge(stored[n], 8 * groups + 16)

        @block.vector
        def _(dve):
            dve.sem_inc(t_copied, 2)
            with dve.Fori(0, groups // 2) as pair:
                g = 2 * pair
                for n in range(2):
                    for u in range(2):
                        dve.wait_ge(t_done, 2 * (g + n) + u + 1)
                        for t in range(2):
                            got = psum[:, 4 + u, 2 * P * t:2 * P * t + 2 * P].rearrange(
                                "p (c j k) -> p j c k", c=2, j=2)[:, :, :, 0:NP]
                            put = cols[:, n, t, 4 * u:4 * u + 4, :].rearrange("p (j c) k -> p j c k", j=2)
                            cp = dve.tensor_copy(put, got)
                        cp.then_inc(t_copied, 1)


def mix_modes(nc, psum, spectrum_dram, mixed_dram, w1_re, w1_im, w2_re, w2_im, part_sign, batch):
    XS = 4
    XY = XS * MODES
    chunks = NX // XS
    M = 2 * batch
    with ExitStack() as ctx:
        def sb(name, shape, dtype=FP32):
            return ctx.enter_context(nc.sbuf_tensor(name, shape, dtype))

        def sem(name):
            return ctx.enter_context(nc.semaphore(name))

        modes = sb("mm_modes", [P, 2, batch, NX, MODES])
        raw = sb("mm_raw", [P, 2, 2, MODES, NP])
        wts = sb("mm_wts", [P, 2, 2, C, XY])
        mixed = sb("mm_mixed", [M, 2, UNIT])
        raw_in = [sem(f"mm_raw_in{n}") for n in range(2)]
        raw_used = sem("mm_raw_used")
        negated_modes = sem("mm_negated_modes")
        w_in = [sem(f"mm_w_in{n}") for n in range(2)]
        w_negated = sem("mm_w_negated")
        u_done, u_copied = sem("mm_u_done"), sem("mm_u_copied")
        stored = [sem(f"mm_stored{n}") for n in range(2)]
        block = ctx.enter_context(nc.Block())
        units = chunks * 2 * XS

        @block.sync
        def _(sp):
            def load_raw(b, n):
                for half in range(2):
                    for plane in range(2):
                        part = plane if half == 0 else 1 - plane
                        sp.dma_start(raw[C * half:C * half + C, n, plane].rearrange("p y k -> p (y k)"),
                                     spectrum_dram[b, :, MODES * part:MODES * part + MODES, :].rearrange(
                                         "c m k -> c (m k)")).then_inc(raw_in[n], 16)
            for b in range(batch):
                if b >= 2:
                    sp.wait_ge(raw_used, b - 1)
                load_raw(b, b % 2)

        @block.gpsimd
        def _(pool):
            for k in range(chunks):
                if k >= 2:
                    pool.wait_ge(u_done, 2 * XS * (k - 1))
                first = k * XS < MODES
                re, im = (w1_re, w1_im) if first else (w2_re, w2_im)
                x0 = k * XS if first else 2 * MODES - (k + 1) * XS
                for half in range(2):
                    for part, src in enumerate((re, im) if half == 0 else (im, re)):
                        pool.dma_start(wts[C * half:C * half + C, k % 2, part],
                                       src[:, :, x0:x0 + XS, :].rearrange("i o x y -> i o (x y)")
                                       ).then_inc(w_in[k % 2], 16)

        @block.vector
        def _(dve):
            def negate(k):
                dve.wait_ge(w_in[k % 2], 64 * (k // 2 + 1))
                w = wts[C:P, k % 2, 0].rearrange("p o q -> p (o q)")
                dve.tensor_scalar(w, w, -1.0, None, ALU.mult).then_inc(w_negated, 1)

            for b in range(batch):
                n = b % 2
                dve.wait_ge(raw_in[n], 64 * (b // 2 + 1))
                cos, sin = raw[:, n, 0], raw[:, n, 1]
                dve.tensor_copy(modes[:, 0, b, 0, :], cos[:, :, 0])
                for plus in range(2):
                    last = MODES if plus else MODES + 1
                    q0 = 1 if plus else MODES
                    put = modes[:, 0, b, q0:q0 + last - 1, :].rearrange("p q y -> p y q")
                    op = dve.scalar_tensor_tensor(put, sin[:, :, MODES + 1:MODES + last],
                                                  part_sign[:, 1 - plus:2 - plus], cos[:, :, 1:last],
                                                  ALU.mult, ALU.add)
                op.then_inc(raw_used, 1)
            dve.wait_ge(raw_used, batch)
            dve.tensor_scalar(modes[:, 1].rearrange("p b q y -> p (b q y)"),
                              modes[:, 0].rearrange("p b q y -> p (b q y)"), -1.0, None, ALU.mult
                              ).then_inc(negated_modes, 1)
            for k in range(chunks):
                negate(k)

        @block.tensor
        def _(pe):
            pe.wait_ge(negated_modes, 1)
            for k in range(chunks):
                pe.wait_ge(w_negated, k + 1)
                for xi in range(XS):
                    q = k * XS + xi
                    x_local = xi if q < MODES else XS - 1 - xi
                    for yh in range(2):
                        u = 2 * q + yh
                        if u >= SLOTS:
                            pe.wait_ge(u_copied, u - SLOTS + 1)
                        for y8 in range(8):
                            y = 8 * yh + y8
                            bank = 2 * (u % SLOTS) + y8 // 4
                            mm = pe.matmul(psum[0:M, bank, P * (y8 % 4):P * (y8 % 4) + P],
                                           modes[:, :, :, q, y].rearrange("p s b -> p (s b)"),
                                           wts[:, k % 2, :, :, MODES * x_local + y].rearrange("p r o -> p (r o)"),
                                           start=True, stop=True)
                        mm.then_inc(u_done, 1)

        @block.scalar
        def _(act):
            out = mixed_dram.rearrange("s b q y r o -> (s b) (q y r o)")
            for u in range(units):
                act.wait_ge(u_done, u + 1)
                if u >= 2:
                    act.wait_ge(stored[u % 2], 16 * (u // 2))
                slot = 2 * (u % SLOTS)
                act.activation(mixed[:, u % 2, :], psum[0:M, slot:slot + 2, :].rearrange("p a q -> p (a q)"),
                               ACT.Copy).then_inc(u_copied, 1)
                act.wait_ge(u_copied, u + 1)
                act.dma_start(out[:, UNIT * u:UNIT * u + UNIT], mixed[:, u % 2, :]).then_inc(stored[u % 2], 16)
            for n in range(2):
                act.wait_ge(stored[n], 16 * (units // 2))


def images(nc, psum, x, mixed_dram, normed_dram, y_out, k, batch):
    order, used = schedule()
    x_c = x.rearrange("b c (f r) w -> b f c (r w)", f=2)
    normed_c = normed_dram.rearrange("b c (f r) w -> b f c (r w)", f=2)
    normed_r = normed_dram.rearrange("b (s o) (f p) w -> b s p (o f) w", p=P, o=2)
    y_r = y_out.rearrange("b (s o) (f p) w -> b s p (o f) w", p=P, o=2)
    with ExitStack() as ctx:
        def sb(name, shape, dtype=FP32):
            return ctx.enter_context(nc.sbuf_tensor(name, shape, dtype))

        def sem(name):
            return ctx.enter_context(nc.semaphore(name))

        image = sb("image", [P, HL * W])
        spec_rows = image[C:C + NY, HL * W // 2:].rearrange("p (r f o) -> p o f r", f=2, o=C)
        conv_rows = image[0:C, HL * W // 2:].rearrange("p (n o) -> p n o", o=C)
        mixed = image[:, :].rearrange("p (r t m) -> p t m r", t=2, m=P)
        xin = k["xin"]
        kept = k["kept"]
        along_w = sb("along_w", [P, 2, UNIT], FP32R)
        freq = sb("freq", [P, 2, UNIT], FP32R)
        along_h = sb("along_h", [P, 2, UNIT], FP32R)
        over = sb("over", [P, 2, UNIT])
        sign = sb("sign", [P, 2, UNIT], BF16)
        resid = sb("resid", [P, 2, UNIT])
        parts = sb("parts", [P, 2 * ROW_UNITS, 6])
        st = sb("st", [P, 12])
        gelu_bias, gn_w, gn_b = k["cols"][:, 0:1], k["cols"][:, 1:2], k["cols"][:, 2:3]

        x_in = [sem(f"x_in{n}") for n in range(X_BUFS)]
        kept_in = [sem(f"kept_in{n}") for n in range(2)]
        conv_copied = sem("conv_copied")
        full = [sem(f"slot{n}_full") for n in range(SLOTS)]
        copied = [sem(f"slot{n}_copied") for n in range(SLOTS)]
        stats_ready = sem("stats_ready")
        rooted = sem("rooted")
        normed = sem("normed")
        spilled = [sem(f"spilled{n}") for n in range(SPILLS)]
        over_made = sem("over_made")
        soft_made = sem("soft_made")
        soft_split = sem("soft_split")
        high = [sem(f"slot{n}_high") for n in range(3)]
        r_in = [sem(f"resid_in{n}") for n in range(2)]
        y_stored = [sem(f"y_stored{n}") for n in range(2)]
        chain = sem("vector_chain")
        block = ctx.enter_context(nc.Block())

        def filled(b, slot, use):
            return b * used[slot] + use + 1

        def freed(b, slot, use):
            return b * used[slot] + use + 1

        def in_sbuf(b, kind, index):
            slot, use = use_of(order, kind, index)
            return copied[slot], b * used[slot] + use + 2

        def slot_cols(slot):
            return psum[:, 2 * slot:2 * slot + 2, :].rearrange("p a q -> p (a q)")

        def x_load(b, i):
            n = i % X_BUFS
            per_image = len(range(n, ROW_UNITS, X_BUFS))
            return n, b * per_image + i // X_BUFS + 1

        @block.gpsimd
        def _(pool):
            with pool.Fori(0, batch) as b:
                for i in range(ROW_UNITS):
                    n = i % X_BUFS
                    if i < X_BUFS:
                        pool.wait_ge(copied[0], freed(b, 0, 0))
                    else:
                        slot, use = use_of(order, "conv", i - X_BUFS)
                        pool.wait_ge(full[slot], filled(b, slot, use))
                    for f in range(2):
                        pool.dma_start(xin[0:C, n, f].rearrange("p r w -> p (r w)"),
                                       x_c[b, f, :, UNIT * i:UNIT * i + UNIT]).then_inc(x_in[n], 16)

        @block.sync
        def _(sp):
            for n in range(2):
                sp.sem_inc(y_stored[n], 16)
            with sp.Fori(0, batch) as b:
                for c in range(KEPTS):
                    if c >= 2:
                        slot, use = use_of(order, "modes_to_rows", (c - 1) * (KEPT_O // 4) - 1)
                        sp.wait_ge(full[slot], filled(b, slot, use))
                    for part in range(2):
                        for r in range(2):
                            src = (0, r) if part == 0 else ((1, 1) if r == 0 else (0, 0))
                            sp.dma_start(kept[NX * part:NX * part + NX, c % 2, :, r, :],
                                         mixed_dram[src[0], b, :, :, src[1], KEPT_O * c:KEPT_O * c + KEPT_O]
                                         ).then_inc(kept_in[c % 2], 16)
                for s in range(SPILLS):
                    sp.wait_ge(normed, b * SPILLS + s + 1)
                    q = SPILL_UNITS * UNIT
                    for f in range(2):
                        sp.dma_start(normed_c[b, f, :, q * s:q * s + q],
                                     image[C * f:C * f + C, q * s:q * s + q]).then_inc(spilled[s], 16)
                for s in range(SPILLS):
                    sp.wait_ge(spilled[s], 32 * b + 32)
                for s in range(STEPS + 1):
                    if s < STEPS:
                        sp.wait_ge(y_stored[s % 2], 16 * (b * (STEPS // 2) + s // 2 + 1))
                        sp.dma_start(resid[:, s % 2, :].rearrange("p (a w) -> p a w", w=W),
                                     normed_r[b, s]).then_inc(r_in[s % 2], 16)
                    if s >= 1:
                        sp.wait_ge(*in_sbuf(b, "inv_w", s - 1))
                        sp.dma_start(y_r[b, s - 1], resid[:, (s - 1) % 2, :].rearrange("p (a w) -> p a w", w=W)
                                     ).then_inc(y_stored[(s - 1) % 2], 16)
            for n in range(2):
                sp.wait_ge(y_stored[n], 8 * batch * STEPS + 16)

        @block.tensor
        def _(pe):
            with pe.Fori(0, batch) as b:
                for kind, i, slot, use in order:
                    pe.wait_ge(copied[slot], freed(b, slot, use))
                    bank = 2 * slot
                    if kind == "modes_to_rows":
                        c, o0 = divmod(4 * i, KEPT_O)
                        if o0 == 0:
                            pe.wait_ge(kept_in[c % 2], 64 * (b * (KEPTS // 2) + c // 2 + 1))
                        for o in range(4):
                            mm = pe.matmul(psum[C:C + NY, bank + o // 2, W * (o % 2):W * (o % 2) + W],
                                           kept[:, c % 2, :, :, o0 + o].rearrange("p y r -> p (y r)"),
                                           k["inv_h"], start=True, stop=True)
                    elif kind == "conv":
                        if i == 0:
                            pe.wait_ge(conv_copied, b + 1)
                            for q in range(C // 4 - SLOTS, C // 4):
                                pe.wait_ge(*in_sbuf(b, "modes_to_rows", q))
                        n, loads = x_load(b, i)
                        pe.wait_ge(x_in[n], 32 * loads)
                        for r in range(ROWS):
                            for f in range(2):
                                at = HL * W // 2 + P * (ROWS * i + r) + C * f
                                mm = pe.matmul(psum[C * f:C * f + C, bank + r // 2, W * (r % 2):W * (r % 2) + W],
                                               image[0:C + NY, at:at + C], xin[:, n, f, r, :],
                                               start=True, stop=True)
                    elif kind == "group":
                        pe.wait_ge(stats_ready, b + 1)
                        mm = pe.matmul(psum[:, bank, 0:2], k["group"], st[:, 2:4], start=True, stop=True)
                    elif kind == "mix":
                        if i % SPILL_UNITS == 0:
                            pe.wait_ge(normed, b * SPILLS + i // SPILL_UNITS + 1)
                        for q in range(8):
                            at = UNIT * i + P * q
                            mm = pe.matmul(psum[:, bank + q // 4, P * (q % 4):P * (q % 4) + P],
                                           image[:, at:at + P], k["mix"], start=True, stop=True)
                    elif kind == "fwd_w":
                        if i == 0:
                            for q in range(ROW_UNITS - SLOTS, ROW_UNITS):
                                pe.wait_ge(*in_sbuf(b, "mix", q))
                        for o in range(2):
                            for f in range(2):
                                for t in range(2):
                                    mm = pe.matmul(psum[:, bank + o, W * f:W * f + W],
                                                   mixed[:, t, C * f + 2 * i + o, :],
                                                   k["wht"][:, t, :].bitcast(FP32),
                                                   start=(t == 0), stop=(t == 1))
                    elif kind == "fwd_h":
                        pe.wait_ge(*in_sbuf(b, "fwd_w", i))
                        for o in range(2):
                            for part in range(2):
                                mm = pe.matmul(psum[:, bank + o, :], k["wht"][:, 0, 0:P],
                                               along_w[:, part, 512 * o:512 * o + 512],
                                               start=(part == 0), stop=(part == 1))
                    elif kind == "inv_h":
                        pe.wait_ge(soft_split, b * STEPS + i + 1)
                        for o in range(2):
                            for t in range(2):
                                for f in range(2):
                                    for part in range(2):
                                        at = 512 * o + W * f + P * t
                                        mm = pe.matmul(psum[:, bank + o, H * t:H * t + H],
                                                       freq[:, part, at:at + P], k["wht"][:, f, :],
                                                       start=(f + part == 0), stop=(f + part == 2))
                    elif kind == "inv_w":
                        pe.wait_ge(*in_sbuf(b, "inv_h", i))
                        for o in range(2):
                            for f in range(2):
                                for t in range(2):
                                    for part in range(2):
                                        at = 512 * o + H * t + P * f
                                        mm = pe.matmul(psum[:, bank + o, W * f:W * f + W],
                                                       along_h[:, part, at:at + P], k["wht"][:, t, :],
                                                       start=(t + part == 0), stop=(t + part == 2))
                    mm.then_inc(full[slot], 1)

        @block.scalar
        def _(act):
            def soft_high(b, i):
                act.wait_ge(soft_made, b * STEPS + i + 1)
                act.activation(freq[:, 0, :], over[:, i % 2, :], ACT.Copy).then_inc(high[1], 1)

            for n in range(SLOTS):
                act.sem_inc(copied[n], 1)
            with act.Fori(0, batch) as b:
                for kind, i, slot, use in order:
                    if kind == "group":
                        act.wait_ge(rooted, 2 * b + 1)
                        act.activation(st[:, 5:6], st[:, 4:5], ACT.Sqrt).then_inc(rooted, 1)
                        continue
                    if kind == "inv_w":
                        continue
                    act.wait_ge(full[slot], filled(b, slot, use))
                    if kind == "fwd_h":
                        if i >= 2:
                            act.wait_ge(soft_split, b * STEPS + i - 1)
                        act.activation(over[:, i % 2, :], slot_cols(slot), ACT.Abs)
                        act.activation(sign[:, i % 2, :], slot_cols(slot), ACT.Sign).then_inc(copied[slot], 1)
                        if i == 0:
                            soft_high(b, 0)
                        continue
                    if kind == "modes_to_rows":
                        out = act.activation(spec_rows[:, 4 * i:4 * i + 4],
                                             slot_cols(slot)[C:C + NY].rearrange("p (o f r) -> p o f r", o=4,
                                                                                        f=2), ACT.Copy)
                    elif kind == "conv":
                        out = act.activation(image[:, UNIT * i:UNIT * i + UNIT], slot_cols(slot), ACT.Gelu,
                                             bias=gelu_bias)
                    elif kind == "mix":
                        if i % SPILL_UNITS == 0:
                            act.wait_ge(spilled[i // SPILL_UNITS], 32 * b + 32)
                        out = act.activation(image[:, UNIT * i:UNIT * i + UNIT], slot_cols(slot), ACT.Copy)
                    elif kind == "fwd_w":
                        act.activation(along_w[:, 0, :], slot_cols(slot), ACT.Copy).then_inc(high[0], 1)
                        continue
                    elif kind == "inv_h":
                        act.activation(along_h[:, 0, :], slot_cols(slot), ACT.Copy).then_inc(high[2], 1)
                        if i + 1 < STEPS:
                            soft_high(b, i + 1)
                        continue
                    out.then_inc(copied[slot], 1)

        @block.vector
        def _(dve):
            LINKS = 9

            def soft_low(b, i):
                dve.wait_ge(high[1], b * STEPS + i + 1)
                dve.tensor_tensor(freq[:, 1, :], over[:, i % 2, :], freq[:, 0, :].bitcast(FP32), ALU.subtract
                                  ).then_inc(soft_split, 1)

            with dve.Fori(0, batch) as b:
                links = 0

                def link(op):
                    nonlocal links
                    links += 1
                    op.then_inc(chain, 1)
                    dve.wait_ge(chain, b * LINKS + links)

                for kind, i, slot, use in order:
                    if kind == "modes_to_rows":
                        if i == 0:
                            dve.wait_ge(full[slot], filled(b, slot, use))
                            dve.tensor_copy(conv_rows, k["conv"].unsqueeze(1).broadcast_to([C, 2 * HL, C])
                                            ).then_inc(conv_copied, 1)
                    elif kind == "conv":
                        dve.wait_ge(*in_sbuf(b, "conv", i))
                        for q in range(2):
                            at = UNIT * i + 512 * q
                            op = dve.bn_stats(parts[:, 2 * i + q, :], image[:, at:at + 512])
                        if i == ROW_UNITS - 1:
                            link(op)
                            dve.memset(st[:, 11:12], GN_EPS)
                            link(dve.bn_aggr(st[:, 0:2], parts[:, :, :].rearrange("p a s -> p (a s)")))
                            link(dve.tensor_tensor(st[:, 6:7], st[:, 0:1], st[:, 0:1], ALU.mult))
                            dve.tensor_copy(st[:, 2:3], st[:, 0:1])
                            dve.tensor_tensor(st[:, 3:4], st[:, 1:2], st[:, 6:7], ALU.add).then_inc(stats_ready, 1)
                    elif kind == "group":
                        dve.wait_ge(full[slot], filled(b, slot, use))
                        dve.tensor_copy(st[:, 7:9], psum[:, 2 * slot, 0:2]).then_inc(copied[slot], 1)
                        dve.wait_ge(*in_sbuf(b, "group", 0))
                        link(dve.tensor_tensor(st[:, 6:7], st[:, 7:8], st[:, 7:8], ALU.mult))
                        link(dve.tensor_tensor(st[:, 6:7], st[:, 8:9], st[:, 6:7], ALU.subtract))
                        dve.scalar_tensor_tensor(st[:, 4:5], st[:, 6:7], 0.0, st[:, 11:12], ALU.max, ALU.add
                                                 ).then_inc(rooted, 1)
                        dve.wait_ge(rooted, 2 * b + 2)
                        link(dve.reciprocal(st[:, 6:7], st[:, 5:6]))
                        link(dve.tensor_tensor(st[:, 9:10], st[:, 6:7], gn_w, ALU.mult))
                        link(dve.tensor_tensor(st[:, 6:7], st[:, 7:8], st[:, 9:10], ALU.mult))
                        link(dve.tensor_tensor(st[:, 10:11], gn_b, st[:, 6:7], ALU.subtract))
                        for s in range(SPILLS):
                            q = SPILL_UNITS * UNIT
                            rows = image[:, q * s:q * s + q]
                            dve.tensor_scalar(rows, rows, st[:, 9:10], st[:, 10:11], ALU.mult, ALU.add
                                              ).then_inc(normed, 1)
                    elif kind == "fwd_h":
                        dve.wait_ge(*in_sbuf(b, "fwd_h", i))
                        both = over[:, i % 2, :].rearrange("p (o q) -> p o q", o=2)
                        dve.tensor_tensor(both, both, k["thr"].unsqueeze(1).broadcast_to([P, 2, 2 * W]),
                                          ALU.subtract).then_inc(over_made, 1)
                        dve.wait_ge(over_made, b * STEPS + i + 1)
                        dve.scalar_tensor_tensor(over[:, i % 2, :], over[:, i % 2, :], 0.0, sign[:, i % 2, :],
                                                 ALU.max, ALU.mult).then_inc(soft_made, 1)
                        if i == 0:
                            soft_low(b, 0)
                    elif kind in ("fwd_w", "inv_h"):
                        to = along_w if kind == "fwd_w" else along_h
                        dve.wait_ge(high[slot], b * STEPS + i + 1)
                        dve.tensor_tensor(to[:, 1, :], slot_cols(slot), to[:, 0, :].bitcast(FP32), ALU.subtract
                                          ).then_inc(copied[slot], 1)
                        if kind == "inv_h" and i + 1 < STEPS:
                            soft_low(b, i + 1)
                    elif kind == "inv_w":
                        dve.wait_ge(full[slot], filled(b, slot, use))
                        dve.wait_ge(r_in[i % 2], 16 * (b * (STEPS // 2) + i // 2 + 1))
                        dve.scalar_tensor_tensor(resid[:, i % 2, :], slot_cols(slot), 1.0 / HW, resid[:, i % 2, :],
                                                 ALU.mult, ALU.add).then_inc(copied[slot], 1)
                assert links == LINKS


def build(nc, a, out, batch):
    with ExitStack() as ctx:
        def sb(name, shape, dtype=FP32):
            return ctx.enter_context(nc.sbuf_tensor(name, shape, dtype))

        spectrum = nc.dram_tensor("spectrum", [batch, C, NY, NP], FP32, kind="Internal").ap()
        mixed_modes = nc.dram_tensor("mixed_modes", [2, batch, NX, MODES, 2, C], FP32, kind="Internal").ap()
        normed = nc.dram_tensor("normed", [batch, C, H, W], FP32, kind="Internal").ap()
        psum = ctx.enter_context(nc.psum_tensor("psum", [P, 8, 512], FP32))
        wht = sb("c_wht", [P, 2, W], FP32R)
        thr = sb("c_thr", [P, 2 * W])
        conv = sb("c_conv", [C, C])
        mix = sb("c_mix", [P, P])
        group = sb("c_group", [P, P])
        xin = sb("xin", [C + NY, X_BUFS, 2, ROWS, W])
        inv_h = sb("c_inv_h", [P, H])
        kept = sb("kept", [P, 2, MODES, 2, KEPT_O])
        cols = sb("c_cols", [P, 3])

        with ExitStack() as early:
            def eb(name, shape):
                return early.enter_context(nc.sbuf_tensor(name, shape, FP32))

            fwd_h = eb("c_fwd_h", [P, 2, NPP])
            fwd_w = eb("c_fwd_w", [P, 2, NY])
            identity = eb("c_identity", [P, P])
            mix_sign = eb("c_mix_sign", [P, P])
            part_sign = eb("c_part_sign", [P, 2])
            wht_in = eb("c_wht_in", [P, 2, W])
            inv_w = eb("c_inv_w", [C + NY, W])
            with nc.semaphore("c_in") as c_in, nc.semaphore("c_made") as c_made, nc.Block() as block:
                loads = [
                    (fwd_h[:, :, :], a["k_fwd_h"]), (fwd_w[:, :, :], a["k_fwd_w"]),
                    (identity[:, :], a["k_identity"]), (mix_sign[:, :], a["k_mix_sign"]),
                    (part_sign[:, :], a["k_part_sign"]), (wht_in[:, :, :], a["k_wht"]),
                    (group[:, :], a["k_group"]), (inv_w[C:, :], a["k_inv_w"]), (inv_h[:, :], a["k_inv_h"]),
                    (thr[:, :].rearrange("p (f w) -> p f w", f=2), a["T"].rearrange("(f p) w -> p f w", p=P)),
                ]
                loads.append((conv[:, :], a["conv_w_t"]))
                for f in range(2):
                    half = slice(C * f, C * f + C)
                    for g in range(2):
                        loads.append((mix[half, C * g:C * g + C], a["mix_w_t"]))
                    for n, name in enumerate(("conv_b", "gn_w", "gn_b")):
                        loads.append((cols[half, n:n + 1], a[name].rearrange("(c n) -> c n", n=1)))

                @block.sync
                def _(sp):
                    for to, source in loads:
                        sp.dma_start(to, source).then_inc(c_in, 16)

                @block.vector
                def _(dve):
                    dve.memset(kept[2 * NX:, :, :, :, :], 0.0)
                    dve.wait_ge(c_in, 16 * len(loads))
                    dve.tensor_tensor(conv[:, :], conv[:, :], identity[0:C, 0:C], ALU.add).then_inc(c_made, 1)
                    dve.tensor_copy(wht[:, :, :], wht_in[:, :, :])
                    for n in range(X_BUFS):
                        dve.tensor_copy(xin[C:, n].rearrange("p f r w -> p (f r) w"),
                                        inv_w[C:, :].unsqueeze(1).broadcast_to([NY, 2 * ROWS, W]))
                    dve.tensor_tensor(mix[:, :], mix[:, :], mix_sign[:, :], ALU.mult).then_inc(c_made, 1)
                    dve.wait_ge(c_made, 2)

            forward_transform(nc, psum, a["x"], spectrum, fwd_h, fwd_w, identity[:, :], batch)
            mix_modes(nc, psum, spectrum, mixed_modes, a["w1_re"], a["w1_im"], a["w2_re"], a["w2_im"],
                      part_sign, batch)
        consts = {"wht": wht, "thr": thr[:, :], "conv": conv[:, :], "mix": mix[:, :], "group": group[:, :],
                  "xin": xin, "inv_h": inv_h[:, :], "cols": cols,
                  "kept": kept}
        images(nc, psum, a["x"], mixed_modes, normed, out, consts, batch)


def constants():
    h = np.arange(H)
    angle = 2 * np.pi / H * np.outer(h, np.arange(MODES + 1))
    fwd_h = np.zeros((H, NPP))
    fwd_h[:, :MODES + 1] = np.cos(angle)
    fwd_h[:, MODES + 1:NP] = np.sin(angle[:, 1:])
    angle = 2 * np.pi / W * np.outer(np.arange(W), np.arange(MODES))
    fwd_w = np.concatenate([np.cos(angle), -np.sin(angle)], axis=1)
    freqs = np.array([q if q < MODES else MODES - 1 - q for q in range(NX)])
    angle = 2 * np.pi / H * np.outer(freqs, h)
    inv_h = np.concatenate([np.cos(angle), np.sin(angle), np.zeros((P - 2 * NX, H))])
    ky = np.arange(MODES)
    angle = 2 * np.pi / W * np.outer(ky, np.arange(W))
    twice = np.where(ky == 0, 1.0, 2.0)[:, None] / HW
    inv_w = np.stack([twice * np.cos(angle), -twice * np.sin(angle)], axis=1).reshape(NY, W)
    wht = np.array([[1.0]])
    while wht.shape[0] < H:
        wht = np.block([[wht, wht], [wht, -wht]])
    quaternion = np.array([[1, -1, -1, -1], [1, 1, -1, 1], [1, 1, 1, -1], [1, -1, 1, 1]])
    sign = np.kron(quaternion.T, np.ones((C // 4, C // 4)))
    row = np.arange(P)
    same = (row[:, None] % C // 2) == (row[None, :] % C // 2)
    part = np.where(row < C, 1.0, -1.0)
    split = lambda m: m.reshape(2, P, -1).transpose(1, 0, 2)
    made = {
        "k_fwd_h": split(fwd_h), "k_fwd_w": split(fwd_w), "k_identity": np.eye(P),
        "k_mix_sign": np.block([[sign, sign], [sign, -sign]]), "k_part_sign": np.stack([part, -part], axis=1),
        "k_wht": split(wht), "k_group": same / 4.0, "k_inv_w": inv_w, "k_inv_h": inv_h,
    }
    return {name: np.ascontiguousarray(m, dtype=np.float32) for name, m in made.items()}


def layout(inputs):
    a = {"x": inputs["x"], "T": inputs["L1_conv_T"]}
    for name in ("w1_re", "w1_im", "w2_re", "w2_im", "conv_b", "gn_w", "gn_b"):
        a[name] = inputs["L0_conv_" + name]
    a["conv_w_t"] = np.asarray(inputs["L0_conv_conv_w"]).T
    r, i, j, k = (np.asarray(inputs["L1_conv_w_" + n]).T for n in "rijk")
    a["mix_w_t"] = np.block([[r, i, j, k], [i, r, k, j], [j, k, r, i], [k, j, i, r]])
    return {name: np.ascontiguousarray(v) for name, v in a.items()} | constants()


def kernel(**inputs):
    import concourse.bacc as bacc
    from concourse.bass_utils import run_bass_kernel_spmd

    a = layout(inputs)
    batch = a["x"].shape[0]
    nc = bacc.Bacc("TRN2", target_bir_lowering=False, num_devices=1)
    aps = {n: nc.dram_tensor(n, v.shape, mybir.dt.from_np(v.dtype), kind="ExternalInput").ap() for n, v in a.items()}
    out = nc.dram_tensor("y", (batch, C, H, W), FP32, kind="ExternalOutput").ap()
    build(nc, aps, out, batch)
    result = run_bass_kernel_spmd(nc, [a], core_ids=[0])
    return result.results[0]["y"]
```

```python
import math
from contextlib import ExitStack

import numpy as np
import concourse.bass as bass
from concourse import mybir

C, H, W = 64, 256, 256
P = 128
HL = H // 2
MODES = 16
NX = 2 * MODES
NP = 2 * MODES + 1
NPP = 64
NY = 2 * MODES
HW = H * W
GN_EPS = 1e-5

FP32 = mybir.dt.float32
FP32R = mybir.dt.float32r
BF16 = mybir.dt.bfloat16
ACT = mybir.ActivationFunctionType
ALU = mybir.AluOpType

UNIT = 1024
SLOTS = 4
SLOT_OF = {"fwd_w": 0, "fwd_h": 1, "inv_h": 2, "inv_w": 3}
ROWS = UNIT // W
ROW_UNITS = HL // ROWS
STEPS = C // 2
X_BUFS, X_ROWS = 8, 2
SHARED = 4
X_LOADS = HL // X_ROWS
EARLY_UNITS = 24
ROWS_OF_VECTOR = (9, 12, 15)
CONV_COPIES = 4
KEPT_O = 16
KEPTS = C // KEPT_O
SPILL_UNITS = 4
SPILLS = ROW_UNITS // SPILL_UNITS


def schedule():
    units, used = [], [0] * SLOTS

    def unit(kind, index, slot):
        units.append((kind, index, slot, used[slot]))
        used[slot] += 1
        return index, slot, used[slot] - 1

    rows = iter([(k, slot) for k, slot in enumerate((0, 0, 1, 0, 1) + (2, 0, 3, 1) * 2 + (2, 0, 3))])

    def taken(n):
        return [unit("modes_to_rows", *next(rows)) for _ in range(n)]

    rows_of_step = {}
    taken(C // 4)
    ahead, units, used[:] = list(units), [], [0] * SLOTS
    rows = iter([(k, slot) for k, slot in enumerate((0, 0, 1, 0, 1) + (2, 0, 3, 1) * 2 + (2, 0, 3))])

    for k in range(ROW_UNITS):
        unit("conv", k, k % SLOTS)
    unit("group", 0, 0)
    for k in range(ROW_UNITS):
        unit("mix", k, k % SLOTS)
    for step in range(STEPS + 3):
        rows_of_step[step] = []
        for kind, lag in (("fwd_h", 1), ("fwd_w", 0), ("inv_w", 3), ("inv_h", 2)):
            if 0 <= step - lag < STEPS:
                unit(kind, step - lag, SLOT_OF[kind])
            elif step >= STEPS:
                rows_of_step[step] += taken(1)
    rows_of_step[STEPS + 3] = taken(C // 4 - 6)
    return ahead, units, used, rows_of_step


def use_of(order, kind, index):
    return next((slot, use) for k, i, slot, use in order if k == kind and i == index)


def forward_transform(nc, psum, x, spectrum_dram, w_fwd_h, w_fwd_w, identity, batch):
    GROUP = 8
    BUFS = 4
    groups = batch * C // GROUP
    x_g = x.rearrange("b (g c) (p t) w -> (b g) p c (t w)", c=GROUP, p=P)
    out_g = spectrum_dram.rearrange("b (g c) m k -> (b g) m c k", c=GROUP)
    with ExitStack() as ctx:
        def sb(name, shape, dtype=FP32):
            return ctx.enter_context(nc.sbuf_tensor(name, shape, dtype))

        def sem(name):
            return ctx.enter_context(nc.semaphore(name))

        xin = sb("p1_x", [P, BUFS, GROUP, 2 * W])
        rows = sb("p1_rows", [P, 4, 512])
        cols = sb("p1_cols", [P, 2, 2, GROUP, NP])
        spec = sb("p1_spec", [NY, 2, GROUP * NP])
        x_in = [sem(f"p1_x_in{n}") for n in range(BUFS)]
        h_done, h_copied = sem("p1_h_done"), sem("p1_h_copied")
        t_done, t_copied = sem("p1_t_done"), sem("p1_t_copied")
        w_done, w_copied = sem("p1_w_done"), sem("p1_w_copied")
        stored = [sem(f"p1_stored{n}") for n in range(2)]
        block = ctx.enter_context(nc.Block())

        @block.sync
        def _(sp):
            for n in range(BUFS):
                sp.dma_start(xin[:, n], x_g[n]).then_inc(x_in[n], 16)
            with sp.Fori(1, groups // BUFS) as turn:
                g = BUFS * turn
                for n in range(BUFS):
                    sp.wait_ge(h_done, 2 * (g + n + 1 - BUFS))
                    sp.dma_start(xin[:, n], x_g[g + n]).then_inc(x_in[n], 16)

        @block.tensor
        def _(pe):
            def along_h(turn, m):
                g, n = BUFS * turn + m - m % 2, m % 2
                pe.wait_ge(x_in[m], 16 * turn + 16)
                for u in range(2):
                    pe.wait_ge(h_copied, 2 * (g + n) + u + 1)
                    for j in range(2):
                        for t in range(2):
                            c0 = 4 * u + 2 * j
                            mm = pe.matmul(psum[NPP * j:NPP * j + NPP, 2 * n + u, :], w_fwd_h[:, t, :],
                                           xin[:, m, c0:c0 + 2, W * t:W * t + W],
                                           start=(t == 0), stop=(t == 1))
                    mm.then_inc(h_done, 1)

            def along_w(turn, last):
                for m in range(BUFS):
                    g, n = BUFS * turn + m - m % 2, m % 2
                    for u in range(2):
                        pe.wait_ge(h_copied, 2 * (g + n) + u + 5)
                        pe.wait_ge(t_copied, 2 * (g + n) + u + 1)
                        for t in range(2):
                            for c in range(2):
                                q = 2 * t + c
                                piece = rows[:, 2 * n + u, W * c + P * t:W * c + P * t + P]
                                mm = pe.transpose(psum[:, 4 + u, P * q:P * q + P], piece, identity)
                        mm.then_inc(t_done, 1)
                    if m + 1 < BUFS:
                        along_h(turn, m + 1)
                    elif not last:
                        along_h(turn + 1, 0)
                    pe.wait_ge(t_copied, 2 * (g + n) + 4)
                    pe.wait_ge(w_copied, g + n + 1)
                    for t in range(2):
                        mm = pe.matmul(psum[0:NY, 6 + n, 0:GROUP * NP], w_fwd_w[:, t, :],
                                       cols[:, n, t].rearrange("p c k -> p (c k)"), start=(t == 0), stop=(t == 1))
                    mm.then_inc(w_done, 1)

            along_h(0, 0)
            with pe.Fori(0, groups // BUFS - 1) as turn:
                along_w(turn, False)
            along_w(groups // BUFS - 1, True)

        @block.scalar
        def _(act):
            act.sem_inc(h_copied, 4)
            act.sem_inc(w_copied, 2)
            for n in range(2):
                act.sem_inc(stored[n], 16)

            def copy_projections(g, n):
                for u in range(2):
                    act.wait_ge(h_done, 2 * (g + n) + u + 1)
                    act.activation(rows[:, 2 * n + u, :], psum[:, 2 * n + u, :], ACT.Copy).then_inc(h_copied, 1)

            def store_spectrum(g, n):
                act.wait_ge(w_done, g + n + 1)
                act.wait_ge(stored[n], 8 * g + 16)
                act.activation(spec[:, n, :], psum[0:NY, 6 + n, 0:GROUP * NP], ACT.Copy).then_inc(w_copied, 1)
                act.wait_ge(w_copied, g + n + 3)
                act.dma_start(out_g[g + n], spec[:, n, :].rearrange("m (c k) -> m c k", k=NP)
                              ).then_inc(stored[n], 16)

            copy_projections(0, 0)
            with act.Fori(0, groups // 2 - 1) as pair:
                g = 2 * pair
                copy_projections(g, 1)
                store_spectrum(g, 0)
                copy_projections(g + 2, 0)
                store_spectrum(g, 1)
            copy_projections(groups - 2, 1)
            store_spectrum(groups - 2, 0)
            store_spectrum(groups - 2, 1)
            for n in range(2):
                act.wait_ge(stored[n], 8 * groups + 16)

        @block.vector
        def _(dve):
            dve.sem_inc(t_copied, 2)
            with dve.Fori(0, groups // 2) as pair:
                g = 2 * pair
                for n in range(2):
                    for u in range(2):
                        dve.wait_ge(t_done, 2 * (g + n) + u + 1)
                        for t in range(2):
                            got = psum[:, 4 + u, 2 * P * t:2 * P * t + 2 * P].rearrange(
                                "p (c j k) -> p j c k", c=2, j=2)[:, :, :, 0:NP]
                            put = cols[:, n, t, 4 * u:4 * u + 4, :].rearrange("p (j c) k -> p j c k", j=2)
                            cp = dve.tensor_copy(put, got)
                        cp.then_inc(t_copied, 1)


def mix_modes(nc, psum, spectrum_dram, mixed_dram, w1_re, w1_im, w2_re, w2_im, batch):
    XS = 8
    XY = XS * MODES
    chunks = NX // XS
    M = 3 * batch
    RAWS = 2
    with ExitStack() as ctx:
        def sb(name, shape, dtype=FP32):
            return ctx.enter_context(nc.sbuf_tensor(name, shape, dtype))

        def sem(name):
            return ctx.enter_context(nc.semaphore(name))

        modes = sb("mm_modes", [P, 3, batch, NX, MODES])
        raw = sb("mm_raw", [P, RAWS, 2, MODES, NP])
        wts = sb("mm_wts", [P, 2, C, XY])
        mixed = sb("mm_mixed", [M, 2, KEPTS, UNIT // KEPTS])
        raw_in = [sem(f"mm_raw_in{n}") for n in range(RAWS)]
        raw_used = sem("mm_raw_used")
        w_in = [sem(f"mm_w_in{n}") for n in range(2)]
        modes_negated = sem("mm_modes_negated")
        u_done, u_copied = sem("mm_u_done"), sem("mm_u_copied")
        stored = [sem(f"mm_stored{n}") for n in range(2)]
        block = ctx.enter_context(nc.Block())

        @block.gpsimd
        def _(pool):
            for k in range(chunks):
                if k >= 2:
                    pool.wait_ge(u_done, XS * (k - 1))
                first = k * XS < MODES
                x0 = k * XS if first else 2 * MODES - (k + 1) * XS
                for part, src in enumerate((w1_re, w1_im) if first else (w2_re, w2_im)):
                    pool.dma_start(wts[C * part:C * part + C, k % 2],
                                   src[:, :, x0:x0 + XS, :].rearrange("i o x y -> i o (x y)")
                                   ).then_inc(w_in[k % 2], 16)

        @block.vector
        def _(dve):
            for b in range(batch):
                n = b % RAWS
                dve.wait_ge(raw_in[n], 32 * (b // RAWS + 1))
                for product in range(2):
                    for half in range(2):
                        rows = slice(C * half, C * half + C)
                        part = half ^ product
                        minus = product == 0 and half == 1
                        cos, sin = raw[rows, n, part], raw[rows, n, 1 - part]
                        put = modes[rows, product, b]
                        dve.tensor_scalar(put[:, 0, :], cos[:, :, 0], -1.0 if minus else 1.0, None, ALU.mult)
                        for negative in range(2):
                            last = MODES + 1 if negative else MODES
                            q0 = MODES if negative else 1
                            to = put[:, q0:q0 + last - 1, :].rearrange("p q y -> p y q")
                            c, s = cos[:, :, 1:last], sin[:, :, MODES + 1:MODES + last]
                            if not minus:
                                less = (part == 1) != (negative == 1)
                                op = dve.tensor_tensor(to, c, s, ALU.subtract if less else ALU.add)
                            elif negative:
                                op = dve.scalar_tensor_tensor(to, c, -1.0, s, ALU.mult, ALU.subtract)
                            else:
                                op = dve.tensor_tensor(to, s, c, ALU.subtract)
                op.then_inc(raw_used, 1)

        @block.tensor
        def _(pe):
            pe.wait_ge(modes_negated, batch)
            for k in range(chunks):
                pe.wait_ge(w_in[k % 2], 32 * (k // 2 + 1))
                for xi in range(XS):
                    q = k * XS + xi
                    x_local = xi if q < MODES else XS - 1 - xi
                    if q >= SLOTS:
                        pe.wait_ge(u_copied, q - SLOTS + 1)
                    for y in range(MODES):
                        bank = 2 * (q % SLOTS) + C * y // 512
                        mm = pe.matmul(psum[0:M, bank, C * y % 512:C * y % 512 + C],
                                       modes[:, :, :, q, y].rearrange("p s b -> p (s b)"),
                                       wts[:, k % 2, :, MODES * x_local + y], start=True, stop=True)
                    mm.then_inc(u_done, 1)

        @block.scalar
        def _(act):
            for b in range(batch):
                act.wait_ge(raw_used, b + 1)
                act.activation(modes[:, 2, b], modes[:, 1, b], ACT.Copy, scale=-1.0).then_inc(modes_negated, 1)
            for q in range(NX):
                act.wait_ge(u_done, q + 1)
                if q >= 2:
                    act.wait_ge(stored[q % 2], 64 * (q // 2))
                slot = 2 * (q % SLOTS)
                got = psum[0:M, slot:slot + 2, :].rearrange("p a (m c o) -> p (a m) c o", c=KEPTS, o=KEPT_O)
                put = mixed[:, q % 2].rearrange("p c (m o) -> p m c o", o=KEPT_O)
                act.activation(put, got, ACT.Copy).then_inc(u_copied, 1)

        @block.sync
        def _(sp):
            for b in range(batch):
                if b >= RAWS:
                    sp.wait_ge(raw_used, b - RAWS + 1)
                for half in range(2):
                    sp.dma_start(raw[C * half:C * half + C, b % RAWS].rearrange("p r y k -> p (r y k)"),
                                 spectrum_dram[b].rearrange("c m k -> c (m k)")).then_inc(raw_in[b % RAWS], 16)
            for q in range(NX):
                sp.wait_ge(u_copied, q + 1)
                for product, times_i, part in ((0, 0, 0), (0, 1, 1), (1, 0, 1), (2, 1, 0)):
                    sp.dma_start(mixed_dram[:, :, times_i, q, part].rearrange("b c y o -> b c (y o)"),
                                 mixed[batch * product:batch * product + batch, q % 2]).then_inc(stored[q % 2], 16)
            for n in range(2):
                sp.wait_ge(stored[n], 64 * (NX // 2))


def images(nc, psum, x, mixed_dram, normed_dram, y_out, k, batch):
    ahead, order, used, rows_of_step = schedule()
    x_c = x.rearrange("b c (f r) w -> b c f (r w)", f=2)
    normed_c = normed_dram.rearrange("b c (f r) w -> b f c (r w)", f=2)
    normed_r = normed_dram.rearrange("b (s o) (p r) w -> b s p o (r w)", p=P, o=2)
    y_r = y_out.rearrange("b (s o) (p r) w -> b s p o (r w)", p=P, o=2)
    with ExitStack() as ctx:
        def sb(name, shape, dtype=FP32):
            return ctx.enter_context(nc.sbuf_tensor(name, shape, dtype))

        def sem(name):
            return ctx.enter_context(nc.semaphore(name))

        image = sb("image", [P, HL * W])
        upper = image[:, HL * W // 2:]
        spec_rows = upper[P - NY:].rearrange("p (r f o) -> p o f r", f=2, o=C)
        conv_rows = upper[0:P - NY].rearrange("p (n o) -> p n o", o=C)
        mixed = image[:, :].rearrange("p (r m o) -> p m o r", m=4, o=C)
        xin = k["xin"]
        kept = k["kept"]
        channels = sb("channels", [P, 2, 4, 2, HL], FP32R)
        along_w = sb("along_w", [P, 2, UNIT], FP32R)
        freq = sb("freq", [P, 2, UNIT], FP32R)
        along_h = sb("along_h", [P, 2, UNIT], FP32R)
        over = sb("over", [P, 2, UNIT])
        sign = sb("sign", [P, 2, UNIT], BF16)
        resid = sb("resid", [P, 2, UNIT])
        x_bufs = [xin[:, n] for n in range(X_BUFS - SHARED)] + [
            t.rearrange("p (f r w) -> p f r w", f=2, w=W)
            for t in (over[:, 0], over[:, 1], sign.rearrange("p s q -> p (s q)").bitcast(FP32), resid[:, 0])]
        parts = resid[:, 1, 0:2 * ROW_UNITS * 6].rearrange("p (u s) -> p u s", s=6)
        st = sb("st", [P, 12])
        gelu_bias, gn_w, gn_b = k["cols"][:, 0:1], k["cols"][:, 1:2], k["cols"][:, 2:3]

        x_in = [sem(f"x_in{n}") for n in range(X_BUFS)]
        kept_in = [sem(f"kept_in{n}") for n in range(2)]
        conv_copied, basis_copied = sem("conv_copied"), sem("basis_copied")
        full = [sem(f"slot{n}_full") for n in range(SLOTS)]
        copied = [sem(f"slot{n}_copied") for n in range(SLOTS)]
        stats_ready = sem("stats_ready")
        rooted = sem("rooted")
        normed = sem("normed")
        spilled = [sem(f"spilled{n}") for n in range(SPILLS)]
        channels_high, channels_low = sem("channels_high"), sem("channels_low")
        abs_made, over_made = sem("abs_made"), sem("over_made")
        soft_made = sem("soft_made")
        soft_split = sem("soft_split")
        high = [sem(f"slot{n}_high") for n in range(3)]
        r_in = [sem(f"resid_in{n}") for n in range(2)]
        y_stored = [sem(f"y_stored{n}") for n in range(2)]
        chain = sem("vector_chain")
        block = ctx.enter_context(nc.Block())

        first = [sum(unit[2] == n for unit in ahead) for n in range(SLOTS)]

        def filled(b, slot, use):
            return b * used[slot] + first[slot] + use + 1

        def freed(b, slot, use):
            return b * used[slot] + first[slot] + use + 1

        def in_sbuf(b, kind, index):
            slot, use = use_of(order, kind, index)
            return copied[slot], b * used[slot] + first[slot] + use + 2

        def slot_cols(slot):
            return psum[:, 2 * slot:2 * slot + 2, :].rearrange("p a q -> p (a q)")

        def psum_of(kind):
            return slot_cols(SLOT_OF[kind])

        def load_kept(sp, m, index, c, wait_full):
            if c >= 2:
                wait_full((c - 1) * (KEPT_O // 4) - 1)
            sp.dma_start(kept[0:2 * NX, c % 2], mixed_dram[index, c].rearrange("s q r y o -> (s q) r y o")
                         ).then_inc(kept_in[c % 2], 16)

        def load_x(sp, index, j):
            q = X_ROWS * W
            sp.dma_start(x_bufs[j % X_BUFS][0:C].rearrange("p f r w -> p f (r w)"),
                         x_c[index, :, :, q * j:q * j + q]).then_inc(x_in[j % X_BUFS], 16)

        def copy_conv(dve, n):
            q = 2 * HL // CONV_COPIES
            dve.tensor_copy(conv_rows[:, q * n:q * n + q, :],
                               k["conv"].unsqueeze(1).broadcast_to([P - NY, q, C])).then_inc(conv_copied, 1)

        def copy_rows(engine, i, slot):
            put = spec_rows[:, 4 * i:4 * i + 4]
            got = slot_cols(slot)[P - NY:].rearrange("p (o f r) -> p o f r", o=4, f=2)
            if engine is nc.vector:
                engine.tensor_copy(put, got).then_inc(copied[slot], 1)
            else:
                engine.activation(put, got, ACT.Copy).then_inc(copied[slot], 1)

        @block.sync
        def _(sp):
            def wait_ahead(i):
                kind, i, slot, use = ahead[i]
                sp.wait_ge(full[slot], use + 1)

            for n in range(2):
                sp.sem_inc(y_stored[n], 16)
            for c in range(KEPTS):
                load_kept(sp, 0, 0, c, wait_ahead)
            for j in range(X_BUFS):
                load_x(sp, 0, j)
            with sp.Fori(0, batch) as b:
                def wait_full(kind, i):
                    slot, use = use_of(order, kind, i)
                    sp.wait_ge(full[slot], filled(b, slot, use))

                def wait_next(i):
                    wait_full("modes_to_rows", i)

                for j in range(X_BUFS, X_LOADS):
                    wait_full("conv", (j - X_BUFS) * X_ROWS // ROWS)
                    load_x(sp, b, j)
                for s in range(SPILLS):
                    sp.wait_ge(normed, b * ROW_UNITS + SPILL_UNITS * (s + 1))
                    q = SPILL_UNITS * UNIT
                    for f in (1, 0):
                        sp.dma_start(normed_c[b, f, :, q * s:q * s + q],
                                     image[C * f:C * f + C, q * s:q * s + q]).then_inc(spilled[s], 16)
                for c in range(2):
                    load_kept(sp, b + 1, (b + 1) % batch, c, wait_next)
                for s in range(SPILLS):
                    sp.wait_ge(spilled[s], 32 * b + 32)
                for s in range(STEPS + 1):
                    if s < STEPS:
                        sp.wait_ge(y_stored[s % 2], 16 * (b * (STEPS // 2) + s // 2 + 1))
                        sp.dma_start(resid[:, s % 2, :].rearrange("p (o q) -> p o q", o=2),
                                     normed_r[b, s]).then_inc(r_in[s % 2], 16)
                    else:
                        load_kept(sp, b + 1, (b + 1) % batch, 2, wait_next)
                    if s >= 1:
                        sp.wait_ge(*in_sbuf(b, "inv_w", s - 1))
                        sp.dma_start(y_r[b, s - 1], resid[:, (s - 1) % 2, :].rearrange("p (o q) -> p o q", o=2)
                                     ).then_inc(y_stored[(s - 1) % 2], 16)
                    if s == STEPS - 2:
                        for j in range(X_BUFS - SHARED):
                            load_x(sp, (b + 1) % batch, j)
                    elif s == STEPS - 1:
                        for j in range(X_BUFS - SHARED, X_BUFS - 1):
                            load_x(sp, (b + 1) % batch, j)
                load_kept(sp, b + 1, (b + 1) % batch, 3, wait_next)
                sp.wait_ge(y_stored[0], 16 * ((b + 1) * (STEPS // 2) + 1))
                load_x(sp, (b + 1) % batch, X_BUFS - 1)
            for n in range(2):
                sp.wait_ge(y_stored[n], 8 * batch * STEPS + 16)
                sp.wait_ge(kept_in[n], 16 * (batch + 1) * (KEPTS // 2))
            for n in range(X_BUFS):
                sp.wait_ge(x_in[n], 16 * (batch * (X_LOADS // X_BUFS) + 1))

        @block.tensor
        def _(pe):
            def modes_to_rows(m, i, slot):
                c, o0 = divmod(4 * i, KEPT_O)
                if o0 == 0:
                    pe.wait_ge(kept_in[c % 2], 16 * (m * (KEPTS // 2) + c // 2 + 1))
                for o in range(4):
                    mm = pe.matmul(psum[P - NY:, 2 * slot + o // 2, W * (o % 2):W * (o % 2) + W],
                                   kept[:, c % 2, :, :, o0 + o].rearrange("p r y -> p (r y)"),
                                   k["inv_h"], start=True, stop=True)
                mm.then_inc(full[slot], 1)

            for kind, i, slot, use in ahead:
                pe.wait_ge(copied[slot], use + 1)
                modes_to_rows(0, i, slot)
            with pe.Fori(0, batch) as b:
                for kind, i, slot, use in order:
                    pe.wait_ge(copied[slot], freed(b, slot, use))
                    bank = 2 * slot
                    if kind == "modes_to_rows":
                        modes_to_rows(b + 1, i, slot)
                        continue
                    if kind == "conv":
                        if i == 0:
                            for n in range(SLOTS):
                                pe.wait_ge(copied[n], freed(b, n, 0))
                            pe.wait_ge(conv_copied, CONV_COPIES * (b + 1))
                        for r in range(ROWS):
                            j, row = divmod(ROWS * i + r, X_ROWS)
                            if row == 0:
                                pe.wait_ge(x_in[j % X_BUFS], 16 * (b * (X_LOADS // X_BUFS) + j // X_BUFS + 1))
                                if X_BUFS - SHARED <= j < X_BUFS:
                                    pe.wait_ge(basis_copied, SHARED * b + j - (X_BUFS - SHARED) + 1)
                            for f in range(2):
                                at = P * (ROWS * i + r) + C * f
                                mm = pe.matmul(psum[C * f:C * f + C, bank + r // 2, W * (r % 2):W * (r % 2) + W],
                                               upper[:, at:at + C], x_bufs[j % X_BUFS][:, f, row, :],
                                               start=True, stop=True)
                    elif kind == "group":
                        pe.wait_ge(stats_ready, b + 1)
                        mm = pe.matmul(psum[:, bank, 0:2], k["group"], st[:, 2:4], start=True, stop=True)
                    elif kind == "mix":
                        pe.wait_ge(normed, b * ROW_UNITS + i + 1)
                        for q in range(8):
                            at = UNIT * i + P * q
                            mm = pe.matmul(psum[:, bank + q // 4, P * (q % 4):P * (q % 4) + P],
                                           image[:, at:at + P], k["mix"], start=True, stop=True)
                    elif kind == "fwd_w":
                        pe.wait_ge(channels_low, b * (STEPS + 1) + i + 2)
                        for o in range(2):
                            for f in range(2):
                                for t in range(2):
                                    for part in range(2):
                                        mm = pe.matmul(psum[:, bank + o, W * f:W * f + W],
                                                       channels[:, part, 2 * t + f, o, :], k["wht"][:, t, :],
                                                       start=(t + part == 0), stop=(t + part == 2))
                    elif kind == "fwd_h":
                        pe.wait_ge(*in_sbuf(b, "fwd_w", i))
                        for o in range(2):
                            for part in range(2):
                                mm = pe.matmul(psum[:, bank + o, :], k["wht"][:, 0, 0:P],
                                               along_w[:, part, 512 * o:512 * o + 512],
                                               start=(part == 0), stop=(part == 1))
                    elif kind == "inv_h":
                        pe.wait_ge(soft_split, b * STEPS + i + 1)
                        for o in range(2):
                            for t in range(2):
                                for f in range(2):
                                    for part in range(2):
                                        at = 512 * o + W * f + P * t
                                        mm = pe.matmul(psum[:, bank + o, H * t:H * t + H],
                                                       freq[:, part, at:at + P], k["wht"][:, f, :],
                                                       start=(f + part == 0), stop=(f + part == 2))
                    elif kind == "inv_w":
                        pe.wait_ge(*in_sbuf(b, "inv_h", i))
                        for o in range(2):
                            for r in range(2):
                                for t in range(2):
                                    for part in range(2):
                                        at = 512 * o + H * t
                                        mm = pe.matmul(psum[:, bank + o, W * r:W * r + W],
                                                       along_h[:, part, at + r:at + H:2], k["wht"][:, t, :],
                                                       start=(t + part == 0), stop=(t + part == 2))
                    mm.then_inc(full[slot], 1)

        @block.scalar
        def _(act):
            def wait_full(b, kind, i):
                slot, use = use_of(order, kind, i)
                act.wait_ge(full[slot], filled(b, slot, use))

            def split_high(i, rows=slice(0, HL)):
                act.activation(channels[:, 0, :, :, rows], mixed[:, :, 2 * i:2 * i + 2, rows], ACT.Copy
                               ).then_inc(channels_high, 1)

            def next_rows(b, i, slot, use):
                act.wait_ge(full[slot], filled(b, slot, use))
                if i == 0:
                    act.wait_ge(channels_low, (STEPS + 1) * (b + 1))
                copy_rows(act, i, slot)

            for n in range(SLOTS):
                act.sem_inc(copied[n], 1)
            for kind, i, slot, use in ahead:
                act.wait_ge(full[slot], use + 1)
                copy_rows(act, i, slot)
            with act.Fori(0, batch) as b:
                for kind, i, slot, use in order:
                    if kind not in ("conv", "group", "mix"):
                        break
                    if kind == "group":
                        act.wait_ge(rooted, 2 * b + 1)
                        act.activation(st[:, 5:6], st[:, 4:5], ACT.Sqrt).then_inc(rooted, 1)
                        continue
                    act.wait_ge(full[slot], filled(b, slot, use))
                    if kind == "conv":
                        act.activation(image[:, UNIT * i:UNIT * i + UNIT], slot_cols(slot), ACT.Gelu,
                                       bias=gelu_bias).then_inc(copied[slot], 1)
                    elif kind == "mix":
                        if i % SPILL_UNITS == 0:
                            act.wait_ge(spilled[i // SPILL_UNITS], 32 * b + 32)
                        act.activation(image[:, UNIT * i:UNIT * i + UNIT], slot_cols(slot), ACT.Copy
                                       ).then_inc(copied[slot], 1)
                        if i in (EARLY_UNITS + SLOTS - 1, ROW_UNITS - 1):
                            q0, q1 = (0, EARLY_UNITS) if i < ROW_UNITS - 1 else (EARLY_UNITS, ROW_UNITS)
                            for q in range(q1 - SLOTS, q1):
                                act.wait_ge(*in_sbuf(b, "mix", q))
                            split_high(0, slice(ROWS * q0, ROWS * q1))
                for step in range(STEPS + 3):
                    if 1 <= step <= STEPS:
                        i = step - 1
                        wait_full(b, "fwd_h", i)
                        if i >= 2:
                            act.wait_ge(soft_split, b * STEPS + i - 1)
                        act.activation(over[:, i % 2, :], psum_of("fwd_h"), ACT.Abs).then_inc(abs_made, 1)
                    if 2 <= step <= STEPS + 1:
                        i = step - 2
                        act.wait_ge(soft_made, b * STEPS + i + 1)
                        act.activation(freq[:, 0, :], over[:, i % 2, :], ACT.Copy).then_inc(high[1], 1)
                    if step < STEPS:
                        wait_full(b, "fwd_w", step)
                        if step + 1 < STEPS:
                            split_high(step + 1)
                        act.activation(along_w[:, 0, :], psum_of("fwd_w"), ACT.Copy).then_inc(high[0], 1)
                    for i, slot, use in rows_of_step.get(step, ()):
                        next_rows(b, i, slot, use)
                    if 1 <= step <= STEPS:
                        act.activation(sign[:, (step - 1) % 2, :], psum_of("fwd_h"), ACT.Sign
                                       ).then_inc(copied[SLOT_OF["fwd_h"]], 1)
                    if 2 <= step <= STEPS + 1:
                        wait_full(b, "inv_h", step - 2)
                        act.activation(along_h[:, 0, :], psum_of("inv_h"), ACT.Copy).then_inc(high[2], 1)
                for i, slot, use in rows_of_step[STEPS + 3]:
                    if i not in ROWS_OF_VECTOR:
                        next_rows(b, i, slot, use)

        @block.gpsimd
        def _(pool):
            def split_low(b, i, rows=slice(0, HL)):
                pool.wait_ge(channels_high, b * (STEPS + 1) + i + (1 if rows.stop < HL else 2))
                pool.tensor_tensor(channels[:, 1, :, :, rows], mixed[:, :, 2 * i:2 * i + 2, rows],
                                   channels[:, 0, :, :, rows].bitcast(FP32), ALU.subtract).then_inc(channels_low, 1)

            with pool.Fori(0, batch) as b:
                split_low(b, 0, slice(0, ROWS * EARLY_UNITS))
                split_low(b, 0, slice(ROWS * EARLY_UNITS, HL))
                for step in range(STEPS + 1):
                    if step >= 1:
                        i = step - 1
                        pool.wait_ge(abs_made, b * STEPS + i + 1)
                        both = over[:, i % 2, :].rearrange("p (o q) -> p o q", o=2)
                        pool.tensor_tensor(both, both, k["thr"].unsqueeze(1).broadcast_to([P, 2, 2 * W]),
                                           ALU.subtract).then_inc(over_made, 1)
                    if step + 1 < STEPS:
                        split_low(b, step + 1)

        @block.vector
        def _(dve):
            LINKS = 7

            def low(to, kind, b, i):
                slot = SLOT_OF[kind]
                dve.wait_ge(high[slot], b * STEPS + i + 1)
                dve.tensor_tensor(to[:, 1, :], slot_cols(slot), to[:, 0, :].bitcast(FP32), ALU.subtract
                                  ).then_inc(copied[slot], 1)

            def copy_basis(n):
                dve.tensor_copy(x_bufs[X_BUFS - SHARED + n][C:], xin[C:, 0]).then_inc(basis_copied, 1)

            for n in range(CONV_COPIES):
                copy_conv(dve, n)
            for n in range(SHARED):
                copy_basis(n)
            with dve.Fori(0, batch) as b:
                links = 0

                def link(op):
                    nonlocal links
                    links += 1
                    op.then_inc(chain, 1)
                    dve.wait_ge(chain, b * LINKS + links)

                for kind, i, slot, use in order:
                    if kind == "conv":
                        dve.wait_ge(*in_sbuf(b, "conv", i))
                        if i == 0:
                            dve.wait_ge(y_stored[1], 16 * (b * (STEPS // 2) + 1))
                        for q in range(2):
                            at = UNIT * i + 512 * q
                            op = dve.bn_stats(parts[:, 2 * i + q, :], image[:, at:at + 512])
                        if i == ROW_UNITS - 1:
                            link(op)
                            dve.memset(st[:, 11:12], GN_EPS)
                            link(dve.bn_aggr(st[:, 2:4], parts.rearrange("p a s -> p (a s)")))
                            dve.scalar_tensor_tensor(st[:, 3:4], st[:, 2:3], st[:, 2:3], st[:, 3:4],
                                                     ALU.mult, ALU.add).then_inc(stats_ready, 1)
                    elif kind == "group":
                        dve.wait_ge(full[slot], filled(b, slot, use))
                        dve.tensor_copy(st[:, 7:9], psum[:, 2 * slot, 0:2]).then_inc(copied[slot], 1)
                        dve.wait_ge(*in_sbuf(b, "group", 0))
                        link(dve.scalar_tensor_tensor(st[:, 6:7], st[:, 7:8], st[:, 7:8], st[:, 8:9],
                                                      ALU.mult, ALU.subtract))
                        link(dve.tensor_scalar(st[:, 6:7], st[:, 6:7], -1.0, 0.0, ALU.mult, ALU.max))
                        dve.tensor_scalar(st[:, 4:5], st[:, 6:7], st[:, 11:12], None, ALU.add).then_inc(rooted, 1)
                        dve.wait_ge(rooted, 2 * b + 2)
                        link(dve.reciprocal(st[:, 6:7], st[:, 5:6]))
                        link(dve.tensor_tensor(st[:, 9:10], st[:, 6:7], gn_w, ALU.mult))
                        link(dve.scalar_tensor_tensor(st[:, 10:11], st[:, 7:8], st[:, 9:10], gn_b,
                                                      ALU.mult, ALU.subtract))
                        for q in range(ROW_UNITS):
                            part = image[:, UNIT * q:UNIT * q + UNIT]
                            dve.tensor_scalar(part, part, st[:, 9:10], st[:, 10:11], ALU.mult, ALU.subtract
                                              ).then_inc(normed, 1)
                for step in range(STEPS + 3):
                    if step < STEPS:
                        low(along_w, "fwd_w", b, step)
                    if 1 <= step <= STEPS:
                        i = step - 1
                        dve.wait_ge(over_made, b * STEPS + i + 1)
                        dve.wait_ge(*in_sbuf(b, "fwd_h", i))
                        dve.scalar_tensor_tensor(over[:, i % 2, :], over[:, i % 2, :], 0.0, sign[:, i % 2, :],
                                                 ALU.max, ALU.mult).then_inc(soft_made, 1)
                    if step >= 3:
                        i, slot = step - 3, SLOT_OF["inv_w"]
                        dve.wait_ge(full[slot], filled(b, slot, use_of(order, "inv_w", i)[1]))
                        dve.wait_ge(r_in[i % 2], 16 * (b * (STEPS // 2) + i // 2 + 1))
                        dve.scalar_tensor_tensor(resid[:, i % 2, :], slot_cols(slot), 1.0 / HW, resid[:, i % 2, :],
                                                 ALU.mult, ALU.add).then_inc(copied[slot], 1)
                    if 2 <= step <= STEPS + 1:
                        low(along_h, "inv_h", b, step - 2)
                    if 1 <= step <= STEPS:
                        i = step - 1
                        dve.wait_ge(high[1], b * STEPS + i + 1)
                        dve.tensor_tensor(freq[:, 1, :], over[:, i % 2, :], freq[:, 0, :].bitcast(FP32),
                                          ALU.subtract).then_inc(soft_split, 1)
                    if step == STEPS:
                        dve.wait_ge(channels_low, (STEPS + 1) * (b + 1))
                        copy_conv(dve, 0)
                    elif step == STEPS + 1:
                        copy_conv(dve, 1)
                    elif step == STEPS + 2:
                        copy_conv(dve, 2)
                for i, slot, use in rows_of_step[STEPS + 3]:
                    if i in ROWS_OF_VECTOR:
                        dve.wait_ge(full[slot], filled(b, slot, use))
                        copy_rows(dve, i, slot)
                        if i == ROWS_OF_VECTOR[0]:
                            copy_conv(dve, 3)
                for n in range(SHARED - 1):
                    copy_basis(n)
                dve.wait_ge(y_stored[0], 16 * ((b + 1) * (STEPS // 2) + 1))
                copy_basis(SHARED - 1)
                assert links == LINKS


def build(nc, a, out, batch):
    with ExitStack() as ctx:
        def sb(name, shape, dtype=FP32):
            return ctx.enter_context(nc.sbuf_tensor(name, shape, dtype))

        spectrum = nc.dram_tensor("spectrum", [batch, C, NY, NP], FP32, kind="Internal").ap()
        mixed_modes = nc.dram_tensor("mixed_modes", [batch, KEPTS, 2, NX, 2, MODES, KEPT_O], FP32, kind="Internal").ap()
        normed = nc.dram_tensor("normed", [batch, C, H, W], FP32, kind="Internal").ap()
        psum = ctx.enter_context(nc.psum_tensor("psum", [P, 8, 512], FP32))
        wht = sb("c_wht", [P, 2, W], FP32R)
        thr = sb("c_thr", [P, 2 * W])
        conv = sb("c_conv", [P - NY, C])
        mix = sb("c_mix", [P, P])
        group = sb("c_group", [P, P])
        xin = sb("xin", [P, X_BUFS - SHARED, 2, X_ROWS, W])
        inv_h = sb("c_inv_h", [P, H])
        kept = sb("kept", [P, 2, 2, MODES, KEPT_O])
        cols = sb("c_cols", [P, 3])

        with ExitStack() as early:
            def eb(name, shape):
                return early.enter_context(nc.sbuf_tensor(name, shape, FP32))

            fwd_h = eb("c_fwd_h", [P, 2, NPP])
            fwd_w = eb("c_fwd_w", [P, 2, NY])
            identity = eb("c_identity", [P, P])
            mix_sign = eb("c_mix_sign", [P, P])
            wht_in = eb("c_wht_in", [P, 2, W])
            inv_w = eb("c_inv_w", [P, W])
            with nc.semaphore("c_in") as c_in, nc.semaphore("c_zero") as c_zero, \
                    nc.semaphore("c_made") as c_made, nc.Block() as block:
                loads = [
                    (fwd_h[:, :, :], a["k_fwd_h"]), (fwd_w[:, :, :], a["k_fwd_w"]),
                    (identity[:, :], a["k_identity"]), (mix_sign[:, :], a["k_mix_sign"]),
                    (wht_in[:, :, :], a["k_wht"]),
                    (group[:, :], a["k_group"]), (inv_w[P - NY:, :], a["k_inv_w"]), (inv_h[:, :], a["k_inv_h"]),
                    (thr[:, :].rearrange("p (f w) -> p f w", f=2), a["T"].rearrange("(f p) w -> p f w", p=P)),
                ]
                loads.append((conv[0:C, :], a["conv_w_t"]))
                for f in range(2):
                    half = slice(C * f, C * f + C)
                    for g in range(2):
                        loads.append((mix[half, C * g:C * g + C], a["mix_w_t"]))
                    for n, name in enumerate(("conv_b", "gn_w", "gn_b")):
                        loads.append((cols[half, n:n + 1], a[name].rearrange("(c n) -> c n", n=1)))

                @block.sync
                def _(sp):
                    for to, source in loads:
                        sp.dma_start(to, source).then_inc(c_in, 16)

                @block.vector
                def _(dve):
                    dve.memset(kept[2 * NX:, :, :, :, :], 0.0)
                    dve.memset(conv[C:, :], 0.0)
                    dve.memset(inv_w[C:P - NY, :], 0.0).then_inc(c_zero, 1)
                    dve.wait_ge(c_in, 16 * len(loads))
                    dve.wait_ge(c_zero, 1)
                    dve.tensor_tensor(conv[0:C, :], conv[0:C, :], identity[0:C, 0:C], ALU.add).then_inc(c_made, 1)
                    dve.tensor_copy(wht[:, :, :], wht_in[:, :, :])
                    for n in range(X_BUFS - SHARED):
                        dve.tensor_copy(xin[C:, n].rearrange("p f r w -> p (f r) w"),
                                        inv_w[C:, :].unsqueeze(1).broadcast_to([P - C, 2 * X_ROWS, W]))
                    dve.tensor_tensor(mix[:, :], mix[:, :], mix_sign[:, :], ALU.mult).then_inc(c_made, 1)
                    dve.wait_ge(c_made, 2)

            forward_transform(nc, psum, a["x"], spectrum, fwd_h, fwd_w, identity[:, :], batch)
            mix_modes(nc, psum, spectrum, mixed_modes, a["w1_re"], a["w1_im"], a["w2_re"], a["w2_im"], batch)
        consts = {"wht": wht, "thr": thr[:, :], "conv": conv[:, :], "mix": mix[:, :], "group": group[:, :],
                  "xin": xin, "inv_h": inv_h[:, :], "cols": cols,
                  "kept": kept}
        images(nc, psum, a["x"], mixed_modes, normed, out, consts, batch)


def constants():
    h = np.arange(H)
    angle = 2 * np.pi / H * np.outer(h, np.arange(MODES + 1))
    fwd_h = np.zeros((H, NPP))
    fwd_h[:, :MODES + 1] = np.cos(angle)
    fwd_h[:, MODES + 1:NP] = np.sin(angle[:, 1:])
    angle = 2 * np.pi / W * np.outer(np.arange(W), np.arange(MODES))
    fwd_w = np.concatenate([np.cos(angle), -np.sin(angle)], axis=1)
    freqs = np.array([q if q < MODES else MODES - 1 - q for q in range(NX)])
    angle = 2 * np.pi / H * np.outer(freqs, h)
    inv_h = np.concatenate([np.cos(angle), np.sin(angle), np.zeros((P - 2 * NX, H))])
    ky = np.arange(MODES)
    angle = 2 * np.pi / W * np.outer(ky, np.arange(W))
    twice = np.where(ky == 0, 1.0, 2.0)[:, None] / HW
    inv_w = np.concatenate([twice * np.cos(angle), -twice * np.sin(angle)])
    wht = np.array([[1.0]])
    while wht.shape[0] < H:
        wht = np.block([[wht, wht], [wht, -wht]])
    quaternion = np.array([[1, -1, -1, -1], [1, 1, -1, 1], [1, 1, 1, -1], [1, -1, 1, 1]])
    sign = np.kron(quaternion.T, np.ones((C // 4, C // 4)))
    row = np.arange(P)
    same = (row[:, None] % C // 2) == (row[None, :] % C // 2)
    split = lambda m: m.reshape(2, P, -1).transpose(1, 0, 2)
    made = {
        "k_fwd_h": fwd_h.reshape(P, 2, NPP), "k_fwd_w": split(fwd_w), "k_identity": np.eye(P),
        "k_mix_sign": np.block([[sign, sign], [sign, -sign]]),
        "k_wht": split(wht), "k_group": same / 4.0, "k_inv_w": inv_w, "k_inv_h": inv_h,
    }
    return {name: np.ascontiguousarray(m, dtype=np.float32) for name, m in made.items()}


def layout(inputs):
    a = {"x": inputs["x"], "T": inputs["L1_conv_T"]}
    for name in ("w1_re", "w1_im", "w2_re", "w2_im", "conv_b", "gn_w", "gn_b"):
        a[name] = inputs["L0_conv_" + name]
    a["conv_w_t"] = np.asarray(inputs["L0_conv_conv_w"]).T
    r, i, j, k = (np.asarray(inputs["L1_conv_w_" + n]).T for n in "rijk")
    a["mix_w_t"] = np.block([[r, i, j, k], [i, r, k, j], [j, k, r, i], [k, j, i, r]])
    return {name: np.ascontiguousarray(v) for name, v in a.items()} | constants()


def kernel(**inputs):
    import concourse.bacc as bacc
    from concourse.bass_utils import run_bass_kernel_spmd

    a = layout(inputs)
    batch = a["x"].shape[0]
    nc = bacc.Bacc("TRN2", target_bir_lowering=False, num_devices=1)
    aps = {n: nc.dram_tensor(n, v.shape, mybir.dt.from_np(v.dtype), kind="ExternalInput").ap() for n, v in a.items()}
    out = nc.dram_tensor("y", (batch, C, H, W), FP32, kind="ExternalOutput").ap()
    build(nc, aps, out, batch)
    result = run_bass_kernel_spmd(nc, [a], core_ids=[0])
    return result.results[0]["y"]
```
